# Optimizing a Trainium2 kernel written in Bass

```python
import numpy as np
import jax
import jax.numpy as jnp

def _softmax(x, axis=-1):
    return jax.nn.softmax(x, axis=axis)

def _gelu(x):
    return jax.nn.gelu(x, approximate=True)

def _silu(x):
    return jax.nn.silu(x)

def _sigmoid(x):
    return jax.nn.sigmoid(x)

def _layernorm(x, axis=-1, eps=1e-05):
    m = jnp.mean(x, axis=axis, keepdims=True)
    v = jnp.var(x, axis=axis, keepdims=True)
    return (x - m) / jnp.sqrt(v + eps)

def _scatter_add(tgt, idx, src, axis=0):
    return tgt.at[idx].add(src)

def _segment_sum(src, seg, n):
    return jax.ops.segment_sum(src, seg, n)
kernel_name = 'mk_macaron_d1_jaxref_r8_ae3ad2'

def setup_inputs(seed: int=0):
    np.random.seed(seed)
    _w = jnp.asarray

    def _L0_attn_setup():
        import jax, jax.numpy as jnp
        import numpy as np
        D_MODEL = 256
        N_HEAD = 16
        SEM_DIM = 128
        GEO_DIM = 128
        ATTN_DIM = 256
        ROPE_BASE = 10000.0

        def _rope(x, base=ROPE_BASE):
            S, d = (x.shape[-2], x.shape[-1])
            inv_freq = 1.0 / base ** (jnp.arange(0, d, 2, dtype=jnp.float32) / d)
            t = jnp.arange(S, dtype=jnp.float32)
            freqs = jnp.einsum('s,f->sf', t, inv_freq)
            cos, sin = (jnp.cos(freqs), jnp.sin(freqs))
            x1, x2 = (x[..., :d // 2], x[..., d // 2:])
            return jnp.concatenate([x1 * cos - x2 * sin, x1 * sin + x2 * cos], axis=-1).astype(x.dtype)

        def _split_heads(y, H):
            B, S, dim = y.shape
            return y.reshape(B, S, H, dim // H).transpose(0, 2, 1, 3)
        key = jax.random.key(seed)
        ks = jax.random.split(key, 7)
        B, S = (2, 256)
        sd = 0.02
        return {'x': jax.random.normal(ks[0], (B, S, D_MODEL), dtype=jnp.float32), 'Wq_sem': jax.random.normal(ks[1], (SEM_DIM, D_MODEL), dtype=jnp.float32) * sd, 'Wk_sem': jax.random.normal(ks[2], (SEM_DIM, D_MODEL), dtype=jnp.float32) * sd, 'Wq_geo': jax.random.normal(ks[3], (GEO_DIM, D_MODEL), dtype=jnp.float32) * sd, 'Wk_geo': jax.random.normal(ks[4], (GEO_DIM, D_MODEL), dtype=jnp.float32) * sd, 'Wv': jax.random.normal(ks[5], (ATTN_DIM, D_MODEL), dtype=jnp.float32) * sd, 'Wo': jax.random.normal(ks[6], (D_MODEL, ATTN_DIM), dtype=jnp.float32) * sd}
    _L0_attn_in = _L0_attn_setup()

    def _L0_ffn_setup():
        import jax, jax.numpy as jnp
        import numpy as np
        L, N, E, H, K = (256, 8, 256, 1024, 8)
        key = jax.random.key(seed)
        ks = jax.random.split(key, 6)
        return {'x': jax.random.normal(ks[0], (L, N, E), dtype=jnp.float32), 'proj1': jax.random.normal(ks[1], (H, E), dtype=jnp.float32) * 0.02, 'proj1_bias': jax.random.normal(ks[2], (H,), dtype=jnp.float32) * 0.02, 'proj2': jax.random.normal(ks[3], (E, H), dtype=jnp.float32) * 0.02, 'proj2_bias': jax.random.normal(ks[4], (E,), dtype=jnp.float32) * 0.02, 'gate_w': jax.random.normal(ks[5], (E, K), dtype=jnp.float32)}
    _L0_ffn_in = _L0_ffn_setup()
    _d = {'L0_attn_x': _L0_attn_in['x'], 'L0_attn_Wq_sem': _L0_attn_in['Wq_sem'], 'L0_attn_Wk_sem': _L0_attn_in['Wk_sem'], 'L0_attn_Wq_geo': _L0_attn_in['Wq_geo'], 'L0_attn_Wk_geo': _L0_attn_in['Wk_geo'], 'L0_attn_Wv': _L0_attn_in['Wv'], 'L0_attn_Wo': _L0_attn_in['Wo'], 'L0_ffn_proj1': _L0_ffn_in['proj1'], 'L0_ffn_proj1_bias': _L0_ffn_in['proj1_bias'], 'L0_ffn_proj2': _L0_ffn_in['proj2'], 'L0_ffn_proj2_bias': _L0_ffn_in['proj2_bias'], 'L0_ffn_gate_w': _L0_ffn_in['gate_w']}
    _x0 = _d['L0_attn_x']
    _d['L0_attn_x'] = jax.random.normal(jax.random.fold_in(jax.random.key(seed), 1), (4, 1024, 256), dtype=_x0.dtype)
    del _x0
    return _d

def reference(L0_attn_x, L0_attn_Wq_sem, L0_attn_Wk_sem, L0_attn_Wq_geo, L0_attn_Wk_geo, L0_attn_Wv, L0_attn_Wo, L0_ffn_proj1, L0_ffn_proj1_bias, L0_ffn_proj2, L0_ffn_proj2_bias, L0_ffn_gate_w):

    def _L0_attn_ref(x, Wq_sem, Wk_sem, Wq_geo, Wk_geo, Wv, Wo):
        import jax, jax.numpy as jnp
        import numpy as np
        D_MODEL = 256
        N_HEAD = 16
        SEM_DIM = 128
        GEO_DIM = 128
        ATTN_DIM = 256
        ROPE_BASE = 10000.0

        def _rope(x, base=ROPE_BASE):
            S, d = (x.shape[-2], x.shape[-1])
            inv_freq = 1.0 / base ** (jnp.arange(0, d, 2, dtype=jnp.float32) / d)
            t = jnp.arange(S, dtype=jnp.float32)
            freqs = jnp.einsum('s,f->sf', t, inv_freq)
            cos, sin = (jnp.cos(freqs), jnp.sin(freqs))
            x1, x2 = (x[..., :d // 2], x[..., d // 2:])
            return jnp.concatenate([x1 * cos - x2 * sin, x1 * sin + x2 * cos], axis=-1).astype(x.dtype)

        def _split_heads(y, H):
            B, S, dim = y.shape
            return y.reshape(B, S, H, dim // H).transpose(0, 2, 1, 3)
        B, S, _ = x.shape
        H = N_HEAD
        q_sem = _split_heads(x @ Wq_sem.T, H)
        k_sem = _split_heads(x @ Wk_sem.T, H)
        q_geo = _rope(_split_heads(x @ Wq_geo.T, H))
        k_geo = _rope(_split_heads(x @ Wk_geo.T, H))
        v = _split_heads(x @ Wv.T, H)
        q = jnp.concatenate([q_sem, q_geo], axis=-1)
        k = jnp.concatenate([k_sem, k_geo], axis=-1)
        scale = 1.0 / jnp.sqrt(jnp.asarray(q.shape[-1], dtype=jnp.float32))
        scores = jnp.einsum('bhqd,bhkd->bhqk', q, k).astype(jnp.float32) * scale
        causal = jnp.tril(jnp.ones((S, S), dtype=bool))
        scores = jnp.where(causal, scores, jnp.finfo(jnp.float32).min)
        attn = jax.nn.softmax(scores, axis=-1).astype(v.dtype)
        out = jnp.einsum('bhqk,bhkd->bhqd', attn, v)
        out = out.transpose(0, 2, 1, 3).reshape(B, S, ATTN_DIM)
        return out @ Wo.T

    def _L0_ffn_ref(x, proj1, proj1_bias, proj2, proj2_bias, gate_w):
        import jax, jax.numpy as jnp
        import numpy as np
        L, N, E, H, K = (256, 8, 256, 1024, 8)
        dst = jnp.argmax(jnp.einsum('lne,ek->lnk', x, gate_w), axis=-1)
        h = jax.nn.gelu(jnp.einsum('lne,he->lnh', x, proj1) + proj1_bias, approximate=False)
        out = jnp.einsum('lnh,eh->lne', h, proj2) + proj2_bias
        del dst
        return out
    x = L0_attn_x
    x = x + 0.5 * _L0_ffn_ref(_layernorm(x, axis=-1), L0_ffn_proj1, L0_ffn_proj1_bias, L0_ffn_proj2, L0_ffn_proj2_bias, L0_ffn_gate_w)
    x = x + _L0_attn_ref(_layernorm(x, axis=-1), L0_attn_Wq_sem, L0_attn_Wk_sem, L0_attn_Wq_geo, L0_attn_Wk_geo, L0_attn_Wv, L0_attn_Wo)
    x = x + 0.5 * _L0_ffn_ref(_layernorm(x, axis=-1), L0_ffn_proj1, L0_ffn_proj1_bias, L0_ffn_proj2, L0_ffn_proj2_bias, L0_ffn_gate_w)
    return x

_drawn_inputs = setup_inputs


def setup_inputs(seed=0):
    import zlib

    import numpy as np

    out = dict(_drawn_inputs(seed))
    spreads = {}
    factors = {'L0_attn_Wq_sem': 8.0,
     'L0_attn_Wk_sem': 8.0,
     'L0_attn_Wq_geo': 8.0,
     'L0_attn_Wk_geo': 8.0,
     'L0_attn_Wv': 6.493,
     'L0_attn_Wo': 6.297,
     'L0_ffn_proj1_bias': 7.984,
     'L0_ffn_proj2_bias': 2.934}
    for name, (base, spread) in spreads.items():
        noise = np.random.default_rng([zlib.crc32(name.encode()), seed]).standard_normal(out[name].shape)
        drawn = base * np.exp(spread * noise) if base else spread * noise
        out[name] = jnp.asarray(drawn.astype(out[name].dtype))
    for name, factor in factors.items():
        out[name] = (out[name] * factor).astype(out[name].dtype)
    return out
```

```python
from contextlib import ExitStack

import numpy as np

import concourse.bass as bass
from concourse import mybir

F32 = mybir.dt.float32
F32R = mybir.dt.float32r
BF16 = mybir.dt.bfloat16
ALU = mybir.AluOpType
ACT = mybir.ActivationFunctionType
AX = mybir.AxisListType

P = 128
B, S, D, HID, H = 4, 1024, 256, 1024, 16
DQ, DV = 16, 16
CH = 512
NCH = B * S // CH
CPB = S // CH
TT = CH // P
KT = D // P
MT = HID // P
GH = 4
HG = H // GH
NG = B * HG
QT = S // P
NPART = 3
Q_BLOCKS = (0, 0, 1, 1, 0, 2)
K_BLOCKS = (0, 1, 0, 1, 2, 0)
NB = len(Q_BLOCKS)
ROWS = NB * DQ
ROWS_M = ROWS + NPART
VW = 32
EPS = 1e-5
SCALE = 0.25
NEG = -3.0e38
RING = 3
PASSES = ((0, 0), (1, 0), (0, 1))

UNITS = [(c, j) for c in range(2) for j in range(4 * (c + 1))]
NU = len(UNITS)


def unit_span(c, j):
    q0 = max(CH * c, P * j)
    return q0, CH * (c + 1) - q0


DIAG = [u for u, (c, j) in enumerate(UNITS) if unit_span(c, j)[0] == P * j]


def score_items():
    items = []
    for i in range(QT):
        for part, k0 in enumerate(range(0, P * (i + 1), CH)):
            w = min(CH, P * (i + 1) - k0)
            per = min(GH, CH // w)
            items += [(i, part, tuple(range(h, h + per)), k0, w) for h in range(0, GH, per)]
    return items


ITEMS = score_items()
NI = len(ITEMS)
FIRST_HALF = sum(i < 4 for i, *_ in ITEMS)
STREAM = [("T1", 0)] + [("S", k) for k in range(FIRST_HALF + 4)] + [("T0", 0)] \
    + [("S", k) for k in range(FIRST_HALF + 4, NI)]
NS = len(STREAM)


def wait(eng, sem, value):
    if not isinstance(value, int) or value > 0:
        eng.wait_ge(sem, value)


def hold(eng, sem, value, passed):
    if not isinstance(value, int) or value > 0:
        eng.wait_ge(sem, value)
        eng.sem_inc(passed, 1)


def macaron(nc, x, w1t, w2t, wqkt, wvt, wot, b1, b2, cos, sin, out):
    ctx = ExitStack()
    with ctx:
        sem = lambda name: ctx.enter_context(nc.semaphore(name))
        sb = lambda c, name, shape, dt=F32: c.enter_context(nc.sbuf_tensor(name, shape, dt))
        ps = lambda c, name, shape, dt=F32: c.enter_context(nc.psum_tensor(name, shape, dt))

        q_stack_d = nc.dram_tensor("q_stack_d", (B, H, ROWS, S), BF16).ap()
        k_stack_d = nc.dram_tensor("k_stack_d", (B, H, ROWS, S), BF16).ap()
        o_d = nc.dram_tensor("o_d", (NG * GH * VW, S), F32).ap()

        x1 = sb(ctx, "x1", [P, NCH * TT, D])
        v_all = sb(ctx, "v_all", [P, B, HG, CPB, TT, GH * DV])
        w1 = sb(ctx, "w1", [P, 2, KT, HID], F32R)
        w2 = sb(ctx, "w2", [P, 2, MT, D], F32R)
        wo = sb(ctx, "wo", [P, 2, KT, D], F32R)
        b1_sb = sb(ctx, "b1_sb", [P, MT])
        hb2 = sb(ctx, "hb2", [P, D])
        ident = sb(ctx, "ident", [P, P])
        neg_half = sb(ctx, "neg_half", [P, TT])

        with ExitStack() as actx:
            wqk = sb(actx, "wqk", [P, 2, KT, 4 * P], F32R)
            wv = sb(actx, "wv", [P, 2, KT, D], F32R)
            cos_sb = sb(actx, "cos_sb", [P, S])
            sin_sb = sb(actx, "sin_sb", [P, S])

            weights = [(w1t, w1, KT, HID), (w2t, w2, MT, D), (wqkt, wqk, KT, 4 * P), (wvt, wv, KT, D),
                       (wot, wo, KT, D)]
            with ExitStack() as c:
                stage = [sb(c, f"stage{n}", [P, kt, w]) for n, (_, _, kt, w) in enumerate(weights)]
                w_loaded = [c.enter_context(nc.semaphore(f"w_loaded{n}")) for n in range(len(weights))]
                small_loaded = c.enter_context(nc.semaphore("small_loaded"))
                w_hi, w_lo = (c.enter_context(nc.semaphore(n)) for n in ("w_hi", "w_lo"))
                consts = c.enter_context(nc.semaphore("consts"))
                hb2_ready = c.enter_context(nc.semaphore("hb2_ready"))
                block = c.enter_context(nc.Block())

                @block.sync
                def _(sp):
                    for n, (src, _, kt, _) in enumerate(weights):
                        sp.dma_start(stage[n][:], src.rearrange("(k p) n -> p k n", p=P)).then_inc(w_loaded[n], 16)
                    sp.dma_start(b1_sb[:], b1).then_inc(small_loaded, 16)
                    sp.dma_start(hb2[:], b2.partition_broadcast(P)).then_inc(small_loaded, 16)
                    sp.dma_start(cos_sb[:], cos).then_inc(small_loaded, 16)
                    sp.dma_start(sin_sb[:], sin).then_inc(small_loaded, 16)
                    sp.wait_ge(small_loaded, 64)

                @block.scalar
                def _(act):
                    for n, (_, dst, _, _) in enumerate(weights):
                        act.wait_ge(w_loaded[n], 16)
                        nc.scalar.activation(dst[:, 0], stage[n][:], ACT.Copy).then_inc(w_hi, 1)
                    act.wait_ge(small_loaded, 64)
                    nc.scalar.activation(hb2[:], hb2[:], ACT.Copy, scale=0.5).then_inc(hb2_ready, 1)

                @block.vector
                def _(dve):
                    for n, (_, dst, _, _) in enumerate(weights):
                        dve.wait_ge(w_hi, n + 1)
                        nc.vector.tensor_tensor(dst[:, 1], stage[n][:], dst[:, 0].bitcast(F32),
                                                ALU.subtract).then_inc(w_lo, 1)

                @block.gpsimd
                def _(pool):
                    nc.gpsimd.memset(ident[:], 0.0).then_inc(consts, 1)
                    nc.gpsimd.memset(neg_half[:], -0.5).then_inc(consts, 1)
                    pool.wait_ge(consts, 2)
                    nc.gpsimd.affine_select(out=ident[:], in_=ident[:], compare_op=ALU.not_equal, fill=1.0,
                                            base=0, pattern=[[-1, P]], channel_multiplier=1).then_inc(consts, 1)

            phase_a(nc, actx, sb, ps, x, x1, v_all, w1, w2, wqk, wv, b1_sb, hb2, ident, neg_half, cos_sb,
                    sin_sb, q_stack_d, k_stack_d)

        with ExitStack() as bctx:
            phase_b(nc, bctx, sb, ps, v_all, ident, q_stack_d, k_stack_d, o_d)

        with ExitStack() as cctx:
            phase_c(nc, cctx, sb, ps, x1, w1, w2, wo, b1_sb, hb2, ident, neg_half, o_d, out)


def mm3(nc, out, w, acts, w_last, k, nk):
    for n, (pw, pa) in enumerate(PASSES):
        last = nc.tensor.matmul(out, w(pw), acts(pa), start=(k == 0 and n == 0),
                                stop=(k == nk - 1 and n == len(PASSES) - 1))
    return last


def phase_a(nc, ctx, sb, ps, x, x1, v_all, w1, w2, wqk, wv, b1_sb, hb2, ident, neg_half, cos_sb, sin_sb,
            q_stack_d, k_stack_d):
    sem = lambda name: ctx.enter_context(nc.semaphore(name))
    x_in = sb(ctx, "x_in", [P, TT, D])
    xb = sb(ctx, "xb", [P, TT, D])
    stats = sb(ctx, "stats", [P, 2, TT, 6])
    mv = sb(ctx, "mv", [P, 2, TT, 2])
    ve = sb(ctx, "ve", [P, 2, TT])
    rstd = sb(ctx, "rstd", [P, 2, TT])
    xn = [sb(ctx, f"xn{n}", [P, TT, D]) for n in range(2)]
    xt = [sb(ctx, f"xt{n}", [P, 2, KT, CH], F32R) for n in range(2)]
    NGB = 4
    g = sb(ctx, "g", [P, NGB, CH])
    h = sb(ctx, "h", [P, 2, MT, CH], F32R)
    rot = sb(ctx, "rot", [P, CH])
    res = sb(ctx, "res", [P, 2, CH])
    parts = sb(ctx, "parts", [P, 2, NPART, CH], BF16)

    hid_ps = ps(ctx, "hid_ps", [P, 2, CH])
    y_ps = ps(ctx, "y_ps", [P, 2, CH])
    tr_ps = ps(ctx, "tr_ps", [P, KT, CH])
    qkv_ps = ps(ctx, "qkv_ps", [P, 2, CH])

    x_loaded = sem("x_loaded")
    stats_done = [sem(f"stats_done{n}") for n in range(2)]
    mean_ready = [sem(f"mean_ready{n}") for n in range(2)]
    ve_ready = [sem(f"ve_ready{n}") for n in range(2)]
    rstd_ready = [sem(f"rstd_ready{n}") for n in range(2)]
    xn_ready = [sem(f"xn_ready{n}") for n in range(2)]
    xt_ps_ready = [sem(f"xt_ps_ready{n}") for n in range(2)]
    xt_hi = [sem(f"xt_hi{n}") for n in range(2)]
    xt_lo = [sem(f"xt_lo{n}") for n in range(2)]
    xb_ready, hid_done, gelu_done, h_hi, h_lo = (sem(n) for n in ("xb_ready", "hid_done", "gelu_done", "h_hi", "h_lo"))
    y_done, x1_ready = sem("y_done"), sem("x1_ready")
    qkv_done, v_evac, rope_step = sem("qkv_done"), sem("v_evac"), sem("rope_step")
    part0, res_ready, part1, part2 = (sem(n) for n in ("part0", "res_ready", "part1", "part2"))
    stored = [sem(f"stored{n}") for n in range(2)]
    PER_STORE = 16 * NB
    dve_passed, pool_passed = sem("a_dve_passed"), sem("a_pool_passed")

    block = ctx.enter_context(nc.Block())

    x_v = x.rearrange("(n a p) d -> n p a d", a=TT, p=P)

    @block.sync
    def _(sp):
        def load(t):
            wait(sp, xn_ready[0], TT * t)
            wait(sp, xb_ready, TT * t)
            sp.dma_start(x_in[:], x_v[bass.ds(t, 1)].rearrange("o p a d -> (o p) a d")).then_inc(x_loaded, 16)

        def store(s):
            for i in range(4):
                dst, blocks = ((q_stack_d, Q_BLOCKS), (k_stack_d, K_BLOCKS))[i // 2]
                half = i % 2
                sp.wait_ge(part2, 4 * s + i + 1)
                for blk, part in enumerate(blocks):
                    for jj in range(2):
                        row = blk * DQ + (2 * half + jj) * 4
                        d = dst[bass.ds(s // CPB, 1), :, row:row + 4, bass.ds((s % CPB) * CH, CH)]
                        i_ = sp.dma_start(d.rearrange("o h d q -> (o h) d q"),
                                          parts[64 * jj:64 * jj + 64, i % 2, part, :])
                        i_.then_inc(stored[i % 2], 16)
        sp.sem_inc(stored[0], 2 * PER_STORE)
        sp.sem_inc(stored[1], 2 * PER_STORE)
        load(0)
        load(1)
        with sp.Fori(1, NCH - 1) as t:
            load(t + 1)
            store(t - 1)
        store(NCH - 2)
        store(NCH - 1)
        for n in range(2):
            sp.wait_ge(stored[n], 2 * PER_STORE * (2 * NCH + 1))

    @block.gpsimd
    def _(pool):
        def rstd_of(n, t):
            hold(pool, mean_ready[n], TT * (t + 1), pool_passed)
            nc.gpsimd.tensor_scalar(ve[:, n], mv[:, n, :, 1], EPS, None, ALU.add).then_inc(ve_ready[n], 1)
            pool.wait_ge(ve_ready[n], t + 1)
            nc.gpsimd.tensor_tensor(rstd[:, n], ve[:, n], neg_half[:], ALU.pow).then_inc(rstd_ready[n], 1)

        def residual_base(t):
            pool.wait_ge(x_loaded, 16 * (t + 1))
            wait(pool, x1_ready, TT * t)
            for a in range(TT):
                nc.gpsimd.tensor_tensor(xb[:, a], x_in[:, a], hb2[:], ALU.add).then_inc(xb_ready, 1)

        rstd_of(0, 0)
        residual_base(0)
        rstd_of(0, 1)
        rstd_of(1, 0)
        residual_base(1)
        with pool.Fori(1, NCH - 1) as t:
            rstd_of(0, t + 1)
            rstd_of(1, t)
            residual_base(t + 1)
        rstd_of(1, NCH - 1)

    @block.scalar
    def _(act):
        def hidden(t, m):
            act.wait_ge(hid_done, MT * t + m + 1)
            wait(act, h_lo, MT * t + m + 1 - NGB)
            nc.scalar.activation(g[:, m % NGB], hid_ps[:, m % 2], ACT.Gelu, bias=b1_sb[:, m:m + 1]).then_inc(gelu_done, 1)

        def upper(t, m):
            act.wait_ge(gelu_done, MT * t + m + 1)
            nc.scalar.activation(h[:, 0, m], g[:, m % NGB], ACT.Copy).then_inc(h_hi, 1)

        def gelus(t, ms):
            for m in ms:
                hidden(t, m)
                if m > ms[0]:
                    upper(t, m - 1)
            upper(t, ms[-1])

        def xt_upper(n, t):
            for k in range(KT):
                act.wait_ge(xt_ps_ready[n], KT * t + k + 1)
                nc.scalar.activation(xt[n][:, 0, k], tr_ps[:, k], ACT.Copy).then_inc(xt_hi[n], 1)

        def qkv_parts(s):
            for i in range(4):
                act.wait_ge(stored[i % 2], 2 * PER_STORE * (2 * s + i // 2 + 1))
                if i % 2 == 0:
                    act.wait_ge(qkv_done, 6 * s + i + 1)
                    src = qkv_ps[:, i % 2]
                else:
                    act.wait_ge(rope_step, 8 * s + 4 * (i // 2) + 4)
                    src = rot[:]
                nc.scalar.activation(parts[:, i % 2, 0], src, ACT.Copy).then_inc(part0, 1)
                act.wait_ge(res_ready, 4 * s + i + 1)
                nc.scalar.activation(parts[:, i % 2, 1], res[:, i % 2], ACT.Copy).then_inc(part1, 1)
            for n in range(2):
                act.wait_ge(qkv_done, 6 * s + 5 + n)
                dst = v_all[:, bass.ds(s // CPB, 1), :, bass.ds(s % CPB, 1), 2 * n:2 * n + 2, :]
                nc.scalar.activation(dst.rearrange("p o g e a c -> p (o g) (e a) c"),
                                     qkv_ps[:, n].rearrange("p (a g c) -> p g a c", a=2, g=HG),
                                     ACT.Copy).then_inc(v_evac, 1)

        def body(t, first=False, last=False):
            gelus(t, range(0, MT // 2))
            if not first:
                xt_upper(1, t - 1)
            gelus(t, range(MT // 2, MT))
            if not last:
                xt_upper(0, t + 1)
            if not first:
                qkv_parts(t - 1)

        act.sem_inc(v_evac, 2)
        xt_upper(0, 0)
        body(0, first=True)
        with act.Fori(1, NCH - 1) as t:
            body(t)
        body(NCH - 1, last=True)
        xt_upper(1, NCH - 1)
        qkv_parts(NCH - 1)

    @block.vector
    def _(dve):
        def src_of(n, t, a):
            return x_in[:, a] if n == 0 else x1[:, bass.ds(TT * t + a, 1), :].rearrange("p o d -> p (o d)")

        def ln_stats(n, t):
            hold(dve, xn_ready[n], TT * t, dve_passed)
            if n:
                hold(dve, x1_ready, TT * (t + 1), dve_passed)
            else:
                hold(dve, x_loaded, 16 * (t + 1), dve_passed)
            for a in range(TT):
                nc.vector.bn_stats(stats[:, n, a], src_of(n, t, a)).then_inc(stats_done[n], 1)
            for a in range(TT):
                hold(dve, stats_done[n], TT * t + a + 1, dve_passed)
                nc.vector.bn_aggr(mv[:, n, a], stats[:, n, a]).then_inc(mean_ready[n], 1)

        def ln_apply(n, t):
            dve.wait_ge(rstd_ready[n], t + 1)
            wait(dve, xt_ps_ready[n], KT * t)
            for a in range(TT):
                nc.vector.tensor_scalar(xn[n][:, a], src_of(n, t, a), mv[:, n, a, 0:1], rstd[:, n, a:a + 1],
                                        ALU.subtract, ALU.mult).then_inc(xn_ready[n], 1)

        def h_lower(t, ms):
            for m in ms:
                dve.wait_ge(h_hi, MT * t + m + 1)
                nc.vector.tensor_tensor(h[:, 1, m], g[:, m % NGB], h[:, 0, m].bitcast(F32),
                                        ALU.subtract).then_inc(h_lo, 1)

        def xt_lower(n, t):
            for k in range(KT):
                dve.wait_ge(xt_hi[n], KT * t + k + 1)
                nc.vector.tensor_tensor(xt[n][:, 1, k], tr_ps[:, k], xt[n][:, 0, k].bitcast(F32),
                                        ALU.subtract).then_inc(xt_lo[n], 1)

        def part_two(s, i):
            dve.wait_ge(part1, 4 * s + i + 1)
            nc.vector.tensor_tensor(parts[:, i % 2, 2], res[:, i % 2], parts[:, i % 2, 1],
                                    ALU.subtract).then_inc(part2, 1)

        def qkv_parts(s):
            for i in range(4):
                if i % 2:
                    dve.wait_ge(qkv_done, 6 * s + i + 1)
                    at = bass.ds((s % CPB) * CH, CH)
                    step = 8 * s + 4 * (i // 2)
                    if i == 3:
                        dve.wait_ge(part2, 4 * s + 2)
                    nc.vector.tensor_tensor(rot[:], qkv_ps[:, 1], cos_sb[:, at], ALU.mult).then_inc(rope_step, 1)
                    nc.vector.tensor_tensor(res[0:64, 1], qkv_ps[64:128, 1], sin_sb[64:128, at], ALU.mult).then_inc(rope_step, 1)
                    nc.vector.tensor_tensor(res[64:128, 1], qkv_ps[0:64, 1], sin_sb[0:64, at], ALU.mult).then_inc(rope_step, 1)
                    dve.wait_ge(rope_step, step + 3)
                    nc.vector.tensor_tensor(rot[:], rot[:], res[:, 1], ALU.add).then_inc(rope_step, 1)
                dve.wait_ge(part0, 4 * s + i + 1)
                src = rot[:] if i % 2 else qkv_ps[:, 0]
                nc.vector.tensor_tensor(res[:, i % 2], src, parts[:, i % 2, 0], ALU.subtract).then_inc(res_ready, 1)
                if i:
                    part_two(s, i - 1)
            part_two(s, 3)
            dve.wait_ge(part2, 4 * s + 4)

        def residual(t):
            dve.wait_ge(xb_ready, TT * (t + 1))
            for a in range(TT):
                dve.wait_ge(y_done, TT * t + 2 * (a // 2) + 2)
                nc.vector.scalar_tensor_tensor(
                    x1[:, bass.ds(TT * t + a, 1), :].rearrange("p o d -> p (o d)"),
                    y_ps[:, a // 2, (a % 2) * D:(a % 2 + 1) * D], 0.5, xb[:, a], ALU.mult,
                    ALU.add).then_inc(x1_ready, 1)

        def body(t, first=False, last=False):
            h_lower(t, range(0, MT // 2))
            if not last:
                ln_stats(0, t + 1)
            if not first:
                xt_lower(1, t - 1)
            if not last:
                ln_apply(0, t + 1)
            h_lower(t, range(MT // 2, MT))
            if not last:
                xt_lower(0, t + 1)
            if not first:
                qkv_parts(t - 1)
            residual(t)
            ln_stats(1, t)
            ln_apply(1, t)

        ln_stats(0, 0)
        ln_apply(0, 0)
        xt_lower(0, 0)
        body(0, first=True)
        with dve.Fori(1, NCH - 1) as t:
            body(t)
        body(NCH - 1, last=True)
        xt_lower(1, NCH - 1)
        qkv_parts(NCH - 1)

    @block.tensor
    def _(pe):
        def transposes(n, t):
            pe.wait_ge(xn_ready[n], TT * (t + 1))
            if n == 0:
                wait(pe, xt_lo[1], KT * (t - 1))
            else:
                wait(pe, xt_lo[0], KT * (t + 2) if not isinstance(t, int) else KT * min(t + 2, NCH))
            for k in range(KT):
                for a in range(TT):
                    last = nc.tensor.transpose(tr_ps[:, k, P * a:P * (a + 1)], xn[n][:, a, P * k:P * (k + 1)], ident[:])
                last.then_inc(xt_ps_ready[n], 1)

        def ffn_up(t, ms):
            pe.wait_ge(xt_lo[0], KT * (t + 1))
            for m in ms:
                wait(pe, gelu_done, MT * t + m - 1)
                for k in range(KT):
                    last = mm3(nc, hid_ps[:, m % 2], lambda p: w1[:, p, k, P * m:P * (m + 1)],
                               lambda p: xt[0][:, p, k], None, k, KT)
                last.then_inc(hid_done, 1)

        def ffn_down(t):
            pe.wait_ge(h_lo, MT * (t + 1))
            wait(pe, x1_ready, TT * t)
            for a in range(TT):
                for k in range(MT):
                    last = mm3(nc, y_ps[:, a // 2, (a % 2) * D:(a % 2 + 1) * D],
                               lambda p: h[:, p, k, P * a:P * (a + 1)], lambda p: w2[:, p, k], None, k, MT)
                last.then_inc(y_done, 1)

        def qkv(s):
            pe.wait_ge(xt_lo[1], KT * (s + 1))
            for m in range(4):
                if m < 2:
                    pe.wait_ge(v_evac, 2 * s + m + 1)
                else:
                    pe.wait_ge(res_ready, 4 * s + m - 1)
                for k in range(KT):
                    last = mm3(nc, qkv_ps[:, m % 2], lambda p: wqk[:, p, k, P * m:P * (m + 1)],
                               lambda p: xt[1][:, p, k], None, k, KT)
                last.then_inc(qkv_done, 1)
            for n in range(2):
                pe.wait_ge(res_ready, 4 * s + 3 + n)
                for a in range(2):
                    for k in range(KT):
                        tile = 2 * n + a
                        last = mm3(nc, qkv_ps[:, n, a * D:(a + 1) * D],
                                   lambda p: xt[1][:, p, k, P * tile:P * (tile + 1)],
                                   lambda p: wv[:, p, k], None, k, KT)
                last.then_inc(qkv_done, 1)

        def body(t, first=False, last=False):
            ffn_up(t, range(0, MT // 2))
            if not first:
                transposes(1, t - 1)
            ffn_up(t, range(MT // 2, MT))
            if not last:
                transposes(0, t + 1)
            if not first:
                qkv(t - 1)
            ffn_down(t)

        transposes(0, 0)
        body(0, first=True)
        with pe.Fori(1, NCH - 1) as t:
            body(t)
        body(NCH - 1, last=True)
        transposes(1, NCH - 1)
        qkv(NCH - 1)


def phase_b(nc, ctx, sb, ps, v_all, ident, q_stack_d, k_stack_d, o_d):
    sem = lambda name: ctx.enter_context(nc.semaphore(name))
    q_st = [sb(ctx, f"q_st{n}", [P, 2, GH, CH], BF16) for n in range(RING)]
    k_st = [sb(ctx, f"k_st{n}", [P, GH, S], BF16) for n in range(RING)]
    va = [sb(ctx, f"va{n}", [P, QT, GH, VW]) for n in range(RING)]
    probs = [sb(ctx, f"probs{n}", [P, GH, CH]) for n in range(RING)]
    ident_bf = sb(ctx, "ident_bf", [P, P], BF16)
    mask_bf = sb(ctx, "mask_bf", [P, P], BF16)
    mask_t_bf = sb(ctx, "mask_t_bf", [P, P], BF16)
    nmax = [sb(ctx, f"nmax{n}", [P, GH, 4]) for n in range(2)]
    pmax = sb(ctx, "pmax", [P, GH, 4, 2])
    n_row = [sb(ctx, f"n_row{n}", [GH * 4, P]) for n in range(2)]
    n_res = [sb(ctx, f"n_res{n}", [GH * 4, P]) for n in range(2)]
    n_part = [sb(ctx, f"n_part{n}", [GH * 4, NPART, P], BF16) for n in range(2)]
    o_sb = [sb(ctx, f"o_sb{n}", [P, CH]) for n in range(2)]

    st_ps = [ps(ctx, f"st_ps{n}", [P, 2, CH]) for n in range(2)]
    s_ps = ps(ctx, "s_ps", [P, 2, CH])
    pv_ps = ps(ctx, "pv_ps", [P, 2, CH])

    loaded = [sem(f"stack_loaded{n}") for n in range(RING)]
    consts, ones_rows, va_ready = sem("b_consts"), sem("ones_rows"), sem("va_ready")
    s_done, max_done, nmax1_ready = sem("s_done"), sem("max_done"), sem("nmax1_ready")
    nt_done, n_row_ready, split_step = sem("nt_done"), sem("n_row_ready"), sem("split_step")
    m_rows = [sem(f"m_rows{n}") for n in range(2)]
    st_done, exp_done, pv_done = (sem(n) for n in ("st_done", "exp_done", "pv_done"))
    o_ready, pool_passed = sem("o_ready"), sem("b_pool_passed")
    o_stored = [sem(f"o_stored{n}") for n in range(2)]
    EXP0, PV0, O0, OS0 = 2, RING, 2, 16
    NCONST = 6 + RING

    qs_v = q_stack_d.rearrange("b (e h) r q -> (b e) r h q", h=GH)
    ks_v = k_stack_d.rearrange("b (e h) r q -> (b e) r h q", h=GH)
    o_v = o_d.rearrange("(g p) q -> g p q", p=P)
    v_v = v_all[:].rearrange("p b g c a w -> p (b g) (c a) w")

    block = ctx.enter_context(nc.Block())

    def groups(eng, body):
        with eng.Fori(0, (NG - 1) // RING) as i:
            for r in range(RING):
                body(RING * i + r, i, r)
        body(NG - 1, (NG - 1) // RING, (NG - 1) % RING, last=True)

    @block.sync
    def _(sp):
        def load(g, r):
            for half in range(2):
                src = qs_v[bass.ds(g, 1), :, :, CH * half:CH * (half + 1)]
                sp.dma_start(q_st[r][0:ROWS, half], src.rearrange("o r h q -> (o r) h q")).then_inc(loaded[r], 16)
            sp.dma_start(k_st[r][0:ROWS], ks_v[bass.ds(g, 1)].rearrange("o r h q -> (o r) h q")).then_inc(loaded[r], 16)

        def max_rows(half, g, r):
            sp.wait_ge(split_step, 4 * (2 * g + half) + 4)
            for part in range(NPART):
                sp.dma_start(q_st[r][ROWS + part:ROWS + part + 1, half].rearrange("p h q -> p (h q)"),
                             n_part[half][:, part, :]).then_inc(m_rows[half], 16)

        def store(c, g):
            sp.wait_ge(o_ready, O0 + 2 * g + c + 1)
            sp.dma_start(o_v[bass.ds(g, 1), :, CH * c:CH * (c + 1)].rearrange("o p q -> (o p) q"),
                         o_sb[c][:]).then_inc(o_stored[c], 16)

        def body(g, i, r, last=False, load_next=True):
            if not last and load_next:
                sp.wait_ge(st_done, 2 * NU * g + 1)
                load(g + 2, (r + 2) % RING)
            max_rows(1, g, r)
            if not last:
                max_rows(0, g + 1, (r + 1) % RING)
            store(0, g)
            store(1, g)

        for c in range(2):
            sp.sem_inc(o_stored[c], OS0)
        load(0, 0)
        load(1, 1)
        max_rows(0, 0, 0)
        n = (NG - 1) // RING
        with sp.Fori(0, n - 1) as i:
            for r in range(RING):
                body(RING * i + r, i, r)
        for r in range(RING):
            g = RING * (n - 1) + r
            body(g, n - 1, r, load_next=g + 2 < NG)
        body(NG - 1, n, (NG - 1) % RING, last=True)
        for c in range(2):
            sp.wait_ge(o_stored[c], OS0 + 16 * NG)

    @block.gpsimd
    def _(pool):
        nc.gpsimd.memset(ident_bf[:], 0.0).then_inc(consts, 1)
        nc.gpsimd.memset(mask_bf[:], 0.0).then_inc(consts, 1)
        nc.gpsimd.memset(mask_t_bf[:], 0.0).then_inc(consts, 1)
        for r in range(RING):
            nc.gpsimd.memset(va[r][:, :, :, DV:VW], 1.0).then_inc(consts, 1)
        pool.wait_ge(consts, 3)
        nc.gpsimd.affine_select(out=mask_t_bf[:], in_=mask_t_bf[:], compare_op=ALU.is_ge, fill=NEG, base=0,
                                pattern=[[1, P]], channel_multiplier=-1).then_inc(consts, 1)
        nc.gpsimd.affine_select(out=ident_bf[:], in_=ident_bf[:], compare_op=ALU.not_equal, fill=1.0, base=0,
                                pattern=[[-1, P]], channel_multiplier=1).then_inc(consts, 1)
        nc.gpsimd.affine_select(out=mask_bf[:], in_=mask_bf[:], compare_op=ALU.is_ge, fill=NEG, base=0,
                                pattern=[[-1, P]], channel_multiplier=1).then_inc(consts, 1)

        def values(g, r):
            nc.gpsimd.tensor_copy(va[r][:, :, :, 0:DV],
                                  v_v[:, bass.ds(g, 1), :, :].rearrange("p o j (h d) -> p (o j) h d", h=GH)
                                  ).then_inc(va_ready, 1)

        def split(half, g):
            k = 2 * g + half
            hold(pool, n_row_ready, k + 1, pool_passed)
            nc.gpsimd.tensor_copy(n_part[half][:, 0], n_row[half][:]).then_inc(split_step, 1)
            pool.wait_ge(split_step, 4 * k + 1)
            nc.gpsimd.tensor_tensor(n_res[half][:], n_row[half][:], n_part[half][:, 0], ALU.subtract).then_inc(split_step, 1)
            hold(pool, split_step, 4 * k + 2, pool_passed)
            nc.gpsimd.tensor_copy(n_part[half][:, 1], n_res[half][:]).then_inc(split_step, 1)
            pool.wait_ge(split_step, 4 * k + 3)
            nc.gpsimd.tensor_tensor(n_part[half][:, 2], n_res[half][:], n_part[half][:, 1], ALU.subtract).then_inc(split_step, 1)

        def body(g, i, r, last=False):
            split(1, g)
            if not last:
                values(g + 1, (r + 1) % RING)
                split(0, g + 1)

        values(0, 0)
        split(0, 0)
        groups(pool, body)

    @block.vector
    def _(dve):
        for r in range(RING):
            nc.vector.memset(k_st[r][ROWS:ROWS_M], 1.0).then_inc(ones_rows, 1)

        def maxima(g, k):
            i, part, heads, _, w = ITEMS[k]
            dve.wait_ge(s_done, NI * g + k + 1)
            slot = (1 + STREAM[1:].index(("S", k))) % 2
            src = s_ps[:, slot, 0:w * len(heads)].rearrange("p (h k) -> p h k", k=w)
            h0, h1 = heads[0], heads[-1] + 1
            if i < 4:
                nc.vector.tensor_reduce(nmax[0][:, h0:h1, i], src, axis=AX.X, op=ALU.max, negate=True).then_inc(max_done, 1)
            else:
                nc.vector.tensor_reduce(pmax[:, h0:h1, i - 4, part], src, axis=AX.X, op=ALU.max).then_inc(max_done, 1)

        def all_maxima(g):
            for k in range(NI):
                maxima(g, k)
            dve.wait_ge(max_done, NI * (g + 1))
            nc.vector.tensor_reduce(nmax[1][:], pmax[:], axis=AX.X, op=ALU.max, negate=True).then_inc(nmax1_ready, 1)

        def body(g, i, r, last=False):
            if not last:
                all_maxima(g + 1)

        all_maxima(0)
        groups(dve, body)

    @block.scalar
    def _(act):
        def row(half, g):
            k = 2 * g + half
            x = STREAM.index((f"T{half}", 0))
            act.wait_ge(nt_done, k + 1)
            nc.scalar.activation(n_row[half][:], s_ps[0:GH * 4, x % 2, 0:P], ACT.Copy).then_inc(n_row_ready, 1)

        def exps(g, u):
            _, w = unit_span(*UNITS[u])
            for hp in range(2):
                act.wait_ge(st_done, 2 * (NU * g + u) + hp + 1)
                if hp == 0:
                    act.wait_ge(pv_done, PV0 + NU * g + u - RING + 1)
                nc.scalar.activation(probs[u % RING][:, 2 * hp:2 * hp + 2, 0:w], st_ps[hp][:, :, 0:w], ACT.Exp,
                                     scale=SCALE).then_inc(exp_done, 1)

        def evacuate(c, g):
            last_unit = 3 if c == 0 else NU - 1
            act.wait_ge(pv_done, PV0 + NU * g + last_unit + 1)
            act.wait_ge(o_stored[c], OS0 + 16 * g)
            nc.scalar.activation(o_sb[c][:], pv_ps[:, c], ACT.Copy).then_inc(o_ready, 1)

        def body(g, i, r, last=False):
            for u in range(NU):
                exps(g, u)
                if u == T_UNIT[1]:
                    row(1, g)
                if u == T_UNIT[0] and not last:
                    row(0, g + 1)
                if u == 5:
                    evacuate(0, g)
            evacuate(1, g)

        act.sem_inc(exp_done, EXP0)
        act.sem_inc(o_ready, O0)
        row(0, 0)
        groups(act, body)

    @block.tensor
    def _(pe):
        def slot_free(g, x):
            y = x - 2
            g, y = (g, y) if y >= 0 else (g - 1, y + NS)
            kind, k = STREAM[y]
            if isinstance(g, int) and (g < 0 or (g == 0 and y == 0)):
                return
            if kind == "S":
                pe.wait_ge(max_done, NI * g + k + 1)
            elif kind == "T0":
                pe.wait_ge(n_row_ready, 2 * g + 1)
            else:
                pe.wait_ge(n_row_ready, 2 * (g - 1) + 2)

        def stream(g, x, r):
            kind, k = STREAM[x]
            slot_free(g, x)
            if kind == "S":
                _, _, heads, k0, w = ITEMS[k]
                i = ITEMS[k][0]
                for n, hd in enumerate(heads):
                    o = s_ps[:, x % 2, n * w:(n + 1) * w]
                    diagonal = k0 + w == P * (i + 1)
                    last = nc.tensor.matmul(o, q_st[r][0:ROWS, i // 4, hd, P * (i % 4):P * (i % 4 + 1)],
                                            k_st[r][0:ROWS, hd, k0:k0 + w], start=True, stop=not diagonal)
                    if diagonal:
                        last = nc.tensor.matmul(o[:, w - P:w], ident_bf[:], mask_bf[:], start=False, stop=True)
                last.then_inc(s_done, 1)
                return
            if kind == "T0":
                pe.wait_ge(max_done, NI * g + FIRST_HALF)
            else:
                pe.wait_ge(nmax1_ready, g)
            nc.tensor.matmul(s_ps[0:GH * 4, x % 2, 0:P], nmax[int(kind[1])][:].rearrange("p h t -> p (h t)"),
                             ident[:], start=True, stop=True).then_inc(nt_done, 1)

        def scores(g, u, r):
            c, j = UNITS[u]
            q0, w = unit_span(c, j)
            if (c, j) in ((0, 0), (1, 0)):
                pe.wait_ge(m_rows[c], 16 * NPART * (g + 1))
            for hp in range(2):
                pe.wait_ge(exp_done, EXP0 + 2 * (NU * g + u) + hp - 1)
                for n in range(2):
                    hd = 2 * hp + n
                    last = nc.tensor.matmul(st_ps[hp][:, n, 0:w], k_st[r][0:ROWS_M, hd, P * j:P * (j + 1)],
                                            q_st[r][0:ROWS_M, c, hd, q0 - CH * c:q0 - CH * c + w],
                                            start=True, stop=u not in DIAG)
                    if u in DIAG:
                        last = nc.tensor.matmul(st_ps[hp][:, n, 0:P], ident_bf[:], mask_t_bf[:], start=False, stop=True)
                last.then_inc(st_done, 1)

        def sums(g, u, r):
            c, j = UNITS[u]
            q0, w = unit_span(c, j)
            pe.wait_ge(exp_done, EXP0 + 2 * (NU * g + u) + 2)
            if j == 0:
                pe.wait_ge(o_ready, O0 + 2 * g + c - 1)
                if c == 0:
                    pe.wait_ge(va_ready, g + 1)
            for hd in range(GH):
                last = nc.tensor.matmul(pv_ps[VW * hd:VW * (hd + 1), c, q0 - CH * c:q0 - CH * c + w],
                                        va[r][:, j, hd, :], probs[u % RING][:, hd, 0:w],
                                        start=j == 0, stop=j == 4 * (c + 1) - 1)
            last.then_inc(pv_done, 1)

        def body(g, i, r, last=False):
            nxt = (r + 1) % RING
            for u in range(NU):
                scores(g, u, r)
                for x in range(u * NS // NU, (u + 1) * NS // NU):
                    if x == 1 and not last:
                        pe.wait_ge(loaded[nxt], 48 * (i + (r + 1) // RING + 1))
                    if not last or x == 0:
                        stream(g + 1, x, nxt)
                if u:
                    sums(g, u - 1, r)
            sums(g, NU - 1, r)

        pe.sem_inc(pv_done, PV0)
        pe.wait_ge(consts, NCONST)
        pe.wait_ge(ones_rows, RING)
        pe.wait_ge(loaded[0], 48)
        for x in range(1, NS):
            stream(0, x, 0)
        groups(pe, body)


T_UNIT = {n: next(u for u in range(NU) if u * NS // NU <= STREAM.index((f"T{n}", 0)) < (u + 1) * NS // NU)
          for n in range(2)}


def phase_c(nc, ctx, sb, ps, x1, w1, w2, wo, b1_sb, hb2, ident, neg_half, o_d, out):
    sem = lambda name: ctx.enter_context(nc.semaphore(name))
    num = sb(ctx, "num", [P, KT, CH])
    den = sb(ctx, "den", [P, KT, CH])
    rden = sb(ctx, "rden", [P, KT, CH])
    att = sb(ctx, "att", [P, KT, CH])
    att_p = sb(ctx, "att_p", [P, 2, KT, CH], F32R)
    xb = sb(ctx, "c_xb", [P, TT, D])
    stats = sb(ctx, "c_stats", [P, TT, 6])
    mv = sb(ctx, "c_mv", [P, TT, 2])
    ve = sb(ctx, "c_ve", [P, TT])
    rstd = sb(ctx, "c_rstd", [P, TT])
    xn = sb(ctx, "c_xn", [P, TT, D])
    xt = sb(ctx, "c_xt", [P, 2, KT, CH], F32R)
    NGB = 4
    g = sb(ctx, "c_g", [P, NGB, CH])
    h = sb(ctx, "c_h", [P, 2, MT, CH], F32R)
    y = sb(ctx, "c_y", [P, TT, D])

    hid_ps = ps(ctx, "c_hid_ps", [P, 2, CH])
    y_ps = ps(ctx, "c_y_ps", [P, 2, CH])
    tr_ps = ps(ctx, "c_tr_ps", [P, KT, CH])
    wo_ps = ps(ctx, "c_wo_ps", [P, 2, CH])

    o_loaded, rden_ready, att_ready, att_hi, att_lo, wo_done, x2_ready = (
        sem(n) for n in ("o_loaded", "rden_ready", "att_ready", "att_hi", "att_lo", "wo_done", "x2_ready"))
    stats_done, mean_ready, ve_ready, rstd_ready, xn_ready = (
        sem(n) for n in ("c_stats_done", "c_mean_ready", "c_ve_ready", "c_rstd_ready", "c_xn_ready"))
    xt_ps_ready, xt_hi, xt_lo, xb_ready = (sem(n) for n in ("c_xt_ps_ready", "c_xt_hi", "c_xt_lo", "c_xb_ready"))
    hid_done, gelu_done, h_hi, h_lo = (sem(n) for n in ("c_hid_done", "c_gelu_done", "c_h_hi", "c_h_lo"))
    y_done, y_ready, y_stored = sem("c_y_done"), sem("c_y_ready"), sem("c_y_stored")
    dve_passed, pool_passed = sem("c_dve_passed"), sem("c_pool_passed")

    o_v = o_d.rearrange("(b k e s r) q -> b k s e r q", b=B, k=KT, s=2, r=DV)
    out_v = out.rearrange("(n a p) d -> n p a d", a=TT, p=P)

    block = ctx.enter_context(nc.Block())

    @block.sync
    def _(sp):
        def load(t):
            wait(sp, att_ready, t)
            for k in range(KT):
                for s, dst in ((0, num), (1, den)):
                    src = o_v[bass.ds(t // CPB, 1), k, s, :, :, bass.ds((t % CPB) * CH, CH)]
                    sp.dma_start(dst[:, k, :], src.rearrange("o e r q -> (o e) r q")).then_inc(o_loaded, 16)

        def store(t):
            sp.wait_ge(y_ready, TT * (t + 1))
            sp.dma_start(out_v[bass.ds(t, 1)].rearrange("o p a d -> (o p) a d"), y[:]).then_inc(y_stored, 16)

        load(0)
        load(1)
        load(2)
        store(0)
        with sp.Fori(1, NCH - 2) as t:
            load(t + 2)
            store(t)
        store(NCH - 2)
        store(NCH - 1)
        sp.wait_ge(y_stored, 16 * NCH)

    @block.gpsimd
    def _(pool):
        def norm(t):
            hold(pool, mean_ready, TT * (t + 1), pool_passed)
            nc.gpsimd.tensor_scalar(ve[:], mv[:, :, 1], EPS, None, ALU.add).then_inc(ve_ready, 1)
            pool.wait_ge(ve_ready, t + 1)
            nc.gpsimd.tensor_tensor(rstd[:], ve[:], neg_half[:], ALU.pow).then_inc(rstd_ready, 1)

        def residual_base(t):
            wait(pool, y_ready, TT * t)
            for a in range(TT):
                nc.gpsimd.tensor_tensor(xb[:, a], x1[:, bass.ds(TT * t + a, 1), :].rearrange("p o d -> p (o d)"),
                                        hb2[:], ALU.add).then_inc(xb_ready, 1)

        norm(0)
        residual_base(0)
        norm(1)
        residual_base(1)
        with pool.Fori(1, NCH - 1) as t:
            norm(t + 1)
            residual_base(t + 1)

    @block.scalar
    def _(act):
        def hidden(t, m):
            act.wait_ge(hid_done, MT * t + m + 1)
            wait(act, h_lo, MT * t + m + 1 - NGB)
            nc.scalar.activation(g[:, m % NGB], hid_ps[:, m % 2], ACT.Gelu, bias=b1_sb[:, m:m + 1]).then_inc(gelu_done, 1)

        def upper(t, m):
            act.wait_ge(gelu_done, MT * t + m + 1)
            nc.scalar.activation(h[:, 0, m], g[:, m % NGB], ACT.Copy).then_inc(h_hi, 1)

        def gelus(t, ms):
            for m in ms:
                hidden(t, m)
                if m > ms[0]:
                    upper(t, m - 1)
            upper(t, ms[-1])

        def xt_upper(t):
            for k in range(KT):
                act.wait_ge(xt_ps_ready, KT * t + k + 1)
                nc.scalar.activation(xt[:, 0, k], tr_ps[:, k], ACT.Copy).then_inc(xt_hi, 1)

        def att_upper(t):
            act.wait_ge(att_ready, t + 1)
            wait(act, wo_done, TT * t)
            nc.scalar.activation(att_p[:, 0], att[:], ACT.Copy).then_inc(att_hi, 1)

        def body(t, nxt=True, second=True):
            gelus(t, range(MT // 2))
            gelus(t, range(MT // 2, MT))
            if nxt:
                xt_upper(t + 1)
            if second:
                att_upper(t + 2)

        att_upper(0)
        xt_upper(0)
        att_upper(1)
        body(0)
        with act.Fori(1, NCH - 2) as t:
            body(t)
        body(NCH - 2, second=False)
        body(NCH - 1, nxt=False, second=False)

    @block.vector
    def _(dve):
        def x1_tile(t, a):
            return x1[:, bass.ds(TT * t + a, 1), :].rearrange("p o d -> p (o d)")

        def attention_rows(t):
            dve.wait_ge(o_loaded, 64 * (t + 1))
            wait(dve, att_lo, t)
            nc.vector.reciprocal(rden[:], den[:]).then_inc(rden_ready, 1)
            dve.wait_ge(rden_ready, t + 1)
            nc.vector.tensor_tensor(att[:], num[:], rden[:], ALU.mult).then_inc(att_ready, 1)

        def att_lower(t):
            dve.wait_ge(att_hi, t + 1)
            nc.vector.tensor_tensor(att_p[:, 1], att[:], att_p[:, 0].bitcast(F32), ALU.subtract).then_inc(att_lo, 1)

        def residual_attention(t):
            for a in range(TT):
                dve.wait_ge(wo_done, TT * t + 2 * (a // 2) + 2)
                nc.vector.tensor_tensor(x1_tile(t, a), wo_ps[:, a // 2, (a % 2) * D:(a % 2 + 1) * D],
                                        x1_tile(t, a), ALU.add).then_inc(x2_ready, 1)

        def layernorm(t):
            hold(dve, xn_ready, TT * t, dve_passed)
            for a in range(TT):
                hold(dve, x2_ready, TT * t + a + 1, dve_passed)
                nc.vector.bn_stats(stats[:, a], x1_tile(t, a)).then_inc(stats_done, 1)
            for a in range(TT):
                hold(dve, stats_done, TT * t + a + 1, dve_passed)
                nc.vector.bn_aggr(mv[:, a], stats[:, a]).then_inc(mean_ready, 1)
            dve.wait_ge(rstd_ready, t + 1)
            wait(dve, xt_ps_ready, KT * t)
            for a in range(TT):
                nc.vector.tensor_scalar(xn[:, a], x1_tile(t, a), mv[:, a, 0:1], rstd[:, a:a + 1],
                                        ALU.subtract, ALU.mult).then_inc(xn_ready, 1)

        def h_lower(t, ms):
            for m in ms:
                dve.wait_ge(h_hi, MT * t + m + 1)
                nc.vector.tensor_tensor(h[:, 1, m], g[:, m % NGB], h[:, 0, m].bitcast(F32),
                                        ALU.subtract).then_inc(h_lo, 1)

        def xt_lower(t):
            for k in range(KT):
                dve.wait_ge(xt_hi, KT * t + k + 1)
                nc.vector.tensor_tensor(xt[:, 1, k], tr_ps[:, k], xt[:, 0, k].bitcast(F32),
                                        ALU.subtract).then_inc(xt_lo, 1)

        def residual(t):
            dve.wait_ge(xb_ready, TT * (t + 1))
            wait(dve, y_stored, 16 * t)
            for a in range(TT):
                dve.wait_ge(y_done, TT * t + 2 * (a // 2) + 2)
                nc.vector.scalar_tensor_tensor(y[:, a], y_ps[:, a // 2, (a % 2) * D:(a % 2 + 1) * D], 0.5,
                                               xb[:, a], ALU.mult, ALU.add).then_inc(y_ready, 1)

        def body(t, nxt=True, second=True):
            h_lower(t, range(MT // 2))
            if nxt:
                residual_attention(t + 1)
                layernorm(t + 1)
            h_lower(t, range(MT // 2, MT))
            if nxt:
                xt_lower(t + 1)
            if second:
                attention_rows(t + 2)
                att_lower(t + 2)
            residual(t)

        attention_rows(0)
        att_lower(0)
        residual_attention(0)
        layernorm(0)
        xt_lower(0)
        attention_rows(1)
        att_lower(1)
        body(0)
        with dve.Fori(1, NCH - 2) as t:
            body(t)
        body(NCH - 2, second=False)
        body(NCH - 1, nxt=False, second=False)

    @block.tensor
    def _(pe):
        def project(t):
            pe.wait_ge(att_lo, t + 1)
            wait(pe, x2_ready, TT * t)
            for a in range(TT):
                for k in range(KT):
                    last = mm3(nc, wo_ps[:, a // 2, (a % 2) * D:(a % 2 + 1) * D],
                               lambda p: att_p[:, p, k, P * a:P * (a + 1)], lambda p: wo[:, p, k], None, k, KT)
                last.then_inc(wo_done, 1)

        def transposes(t):
            pe.wait_ge(xn_ready, TT * (t + 1))
            for k in range(KT):
                for a in range(TT):
                    last = nc.tensor.transpose(tr_ps[:, k, P * a:P * (a + 1)], xn[:, a, P * k:P * (k + 1)], ident[:])
                last.then_inc(xt_ps_ready, 1)

        def ffn_up(t, ms):
            pe.wait_ge(xt_lo, KT * (t + 1))
            for m in ms:
                wait(pe, gelu_done, MT * t + m - 1)
                for k in range(KT):
                    last = mm3(nc, hid_ps[:, m % 2], lambda p: w1[:, p, k, P * m:P * (m + 1)],
                               lambda p: xt[:, p, k], None, k, KT)
                last.then_inc(hid_done, 1)

        def ffn_down(t):
            pe.wait_ge(h_lo, MT * (t + 1))
            wait(pe, y_ready, TT * t)
            for a in range(TT):
                for k in range(MT):
                    last = mm3(nc, y_ps[:, a // 2, (a % 2) * D:(a % 2 + 1) * D],
                               lambda p: h[:, p, k, P * a:P * (a + 1)], lambda p: w2[:, p, k], None, k, MT)
                last.then_inc(y_done, 1)

        def body(t, nxt=True):
            ffn_up(t, range(MT // 2))
            if nxt:
                project(t + 1)
            ffn_up(t, range(MT // 2, MT))
            if nxt:
                transposes(t + 1)
            ffn_down(t)

        project(0)
        transposes(0)
        body(0)
        with pe.Fori(1, NCH - 1) as t:
            body(t)
        body(NCH - 1, nxt=False)



def rope_tables():
    inv_freq = (np.float32(1.0) / np.float32(10000.0) ** (np.arange(0, 8, 2, dtype=np.float32) / np.float32(8)))
    ang = np.arange(S, dtype=np.float32)[None, :] * inv_freq.astype(np.float32)[:, None]
    rows = np.arange(P) % 4
    sign = np.where(np.arange(P) < P // 2, 1.0, -1.0).astype(np.float32)
    return np.cos(ang)[rows], np.sin(ang)[rows] * sign[:, None]


def kernel(**inputs):
    import concourse.bacc as bacc
    from concourse.bass_utils import run_bass_kernel_spmd

    a = {k[3:]: np.asarray(v) for k, v in inputs.items()}

    def rows(w):
        return w.reshape(H, 2, 4, D).transpose(1, 0, 2, 3).reshape(P, D)

    wqk = np.concatenate([rows(a[n]) for n in ("attn_Wq_sem", "attn_Wq_geo", "attn_Wk_sem", "attn_Wk_geo")])
    cos, sin = rope_tables()
    arrays = {
        "x": a["attn_x"].reshape(B * S, D),
        "w1t": a["ffn_proj1"].T, "w2t": a["ffn_proj2"].T, "wqkt": wqk.T, "wvt": a["attn_Wv"].T,
        "wot": a["attn_Wo"].T, "b1": a["ffn_proj1_bias"].reshape(MT, P).T, "b2": a["ffn_proj2_bias"],
        "cos": cos, "sin": sin,
    }
    arrays = {f"in_{k}": np.ascontiguousarray(v) for k, v in arrays.items()}
    nc = bacc.Bacc("TRN2", target_bir_lowering=False, num_devices=1)
    args = [nc.dram_tensor(k, v.shape, mybir.dt.from_np(v.dtype), kind="ExternalInput").ap() for k, v in arrays.items()]
    args.append(nc.dram_tensor("out_0", (B * S, D), F32, kind="ExternalOutput").ap())
    macaron(nc, *args)
    r = run_bass_kernel_spmd(nc, [arrays], core_ids=[0])
    return r.results[0]["out_0"].reshape(B, S, D)
```

```python
from contextlib import ExitStack

import numpy as np

import concourse.bass as bass
from concourse import mybir

F32 = mybir.dt.float32
F32R = mybir.dt.float32r
BF16 = mybir.dt.bfloat16
ALU = mybir.AluOpType
ACT = mybir.ActivationFunctionType
AX = mybir.AxisListType

P = 128
B, S, D, HID, H = 4, 1024, 256, 1024, 16
DQ, DV = 16, 16
CH = 512
NCH = B * S // CH
CPB = S // CH
TT = CH // P
KT = D // P
MT = HID // P
GH = 4
HG = H // GH
NG = B * HG
QT = S // P
NPART = 3
Q_BLOCKS = (0, 0, 1, 1, 0, 2)
K_BLOCKS = (0, 1, 0, 1, 2, 0)
NB = len(Q_BLOCKS)
ROWS = NB * DQ
ROWS_M = ROWS + NPART
VW = 32
EPS = 1e-5
SCALE = 0.25
NEG = -3.0e38
RING = 3
PASSES = ((0, 0), (1, 0), (0, 1))

UNITS = [(c, j) for c in range(2) for j in range(4 * (c + 1))]
NU = len(UNITS)


def unit_span(c, j):
    q0 = max(CH * c, P * j)
    return q0, CH * (c + 1) - q0


DIAG = [u for u, (c, j) in enumerate(UNITS) if unit_span(c, j)[0] == P * j]


def score_items():
    items = []
    for i in range(QT):
        for part, k0 in enumerate(range(0, P * (i + 1), CH)):
            w = min(CH, P * (i + 1) - k0)
            per = min(GH, CH // w)
            items += [(i, part, tuple(range(h, h + per)), k0, w) for h in range(0, GH, per)]
    return items


ITEMS = score_items()
NI = len(ITEMS)
FIRST_HALF = sum(i < 4 for i, *_ in ITEMS)
STREAM = [("T1", 0)] + [("S", k) for k in range(FIRST_HALF + 4)] + [("T0", 0)] \
    + [("S", k) for k in range(FIRST_HALF + 4, NI)]
NS = len(STREAM)


def wait(eng, sem, value):
    if not isinstance(value, int) or value > 0:
        eng.wait_ge(sem, value)


def hold(eng, sem, value, passed):
    if not isinstance(value, int) or value > 0:
        eng.wait_ge(sem, value)
        eng.sem_inc(passed, 1)


def macaron(nc, x, w1t, w2t, wqkt, wvt, wot, b1, b2, cos, sin, out):
    ctx = ExitStack()
    with ctx:
        sem = lambda name: ctx.enter_context(nc.semaphore(name))
        sb = lambda c, name, shape, dt=F32: c.enter_context(nc.sbuf_tensor(name, shape, dt))
        ps = lambda c, name, shape, dt=F32: c.enter_context(nc.psum_tensor(name, shape, dt))

        q_parts_d = nc.dram_tensor("q_parts_d", (B, NPART, H * DQ, S), BF16).ap()
        k_parts_d = nc.dram_tensor("k_parts_d", (B, NPART, H * DQ, S), BF16).ap()
        o_d = nc.dram_tensor("o_d", (NG * GH * VW, S), F32).ap()

        x1 = sb(ctx, "x1", [P, NCH * TT, D])
        v_all = sb(ctx, "v_all", [P, B, HG, CPB, TT, GH * DV])
        w1 = sb(ctx, "w1", [P, 2, KT, HID], F32R)
        w2 = sb(ctx, "w2", [P, 2, MT, D], F32R)
        wo = sb(ctx, "wo", [P, 2, KT, D], F32R)
        b1_sb = sb(ctx, "b1_sb", [P, MT])
        hb2 = sb(ctx, "hb2", [P, D])
        ident = sb(ctx, "ident", [P, P])
        neg_half = sb(ctx, "neg_half", [P, TT])

        with ExitStack() as actx:
            wqk = sb(actx, "wqk", [P, 2, KT, 4 * P], F32R)
            wv = sb(actx, "wv", [P, 2, KT, D], F32R)
            cos_sb = sb(actx, "cos_sb", [P, S])
            sin_sb = sb(actx, "sin_sb", [P, S])

            weights = [(w1t, w1, KT, HID), (w2t, w2, MT, D), (wqkt, wqk, KT, 4 * P), (wvt, wv, KT, D),
                       (wot, wo, KT, D)]
            small = [(b1_sb[:], b1), (hb2[:], b2.partition_broadcast(P)), (cos_sb[:], cos), (sin_sb[:], sin)]
            phase_a(nc, actx, sb, ps, weights, small, x, x1, v_all, w1, w2, wqk, wv, b1_sb, hb2, ident, neg_half, cos_sb,
                    sin_sb, q_parts_d, k_parts_d)

        with ExitStack() as bctx:
            phase_b(nc, bctx, sb, ps, v_all, ident, q_parts_d, k_parts_d, o_d)

        with ExitStack() as cctx:
            phase_c(nc, cctx, sb, ps, x1, w1, w2, wo, b1_sb, hb2, ident, neg_half, o_d, out)


def mm3(nc, out, w, acts, w_last, k, nk):
    for n, (pw, pa) in enumerate(PASSES):
        last = nc.tensor.matmul(out, w(pw), acts(pa), start=(k == 0 and n == 0),
                                stop=(k == nk - 1 and n == len(PASSES) - 1))
    return last


def phase_a(nc, ctx, sb, ps, weights, small, x, x1, v_all, w1, w2, wqk, wv, b1_sb, hb2, ident, neg_half, cos_sb, sin_sb,
            q_parts_d, k_parts_d):
    sem = lambda name: ctx.enter_context(nc.semaphore(name))
    x_in = sb(ctx, "x_in", [P, TT, D])
    stats = sb(ctx, "stats", [P, 2, TT, 6])
    mv = sb(ctx, "mv", [P, 2, TT, 2])
    rstd = sb(ctx, "rstd", [P, 2, TT])
    xn = sb(ctx, "xn", [P, TT, D])
    xt = [sb(ctx, f"xt{n}", [P, 2, KT, CH], F32R) for n in range(2)]
    NGB = 4
    g = sb(ctx, "g", [P, NGB, CH])
    with ExitStack() as c:
        stage = [sb(c, f"stage{n}", [P, kt, w]) for n, (_, _, kt, w) in enumerate(weights)]
    h = sb(ctx, "h", [P, 2, MT, CH], F32R)
    rot = sb(ctx, "rot", [P, CH])
    res = sb(ctx, "res", [P, 2, CH])
    parts = sb(ctx, "parts", [P, 4, NPART, CH], BF16)

    hid_ps = ps(ctx, "hid_ps", [P, 2, CH])
    y_ps = ps(ctx, "y_ps", [P, 2, CH])
    tr_ps = ps(ctx, "tr_ps", [P, KT, CH])
    qkv_ps = ps(ctx, "qkv_ps", [P, 2, CH])

    x_loaded = sem("x_loaded")
    stats_done = [sem(f"stats_done{n}") for n in range(2)]
    mean_ready = [sem(f"mean_ready{n}") for n in range(2)]
    ve_ready = [sem(f"ve_ready{n}") for n in range(2)]
    rstd_ready = [sem(f"rstd_ready{n}") for n in range(2)]
    xn_ready = [sem(f"xn_ready{n}") for n in range(2)]
    xt_ps_ready = [sem(f"xt_ps_ready{n}") for n in range(2)]
    xt_hi = [sem(f"xt_hi{n}") for n in range(2)]
    xt_lo = [sem(f"xt_lo{n}") for n in range(2)]
    base_ready, hid_done, gelu_done, h_hi, h_lo = (sem(n) for n in ("base_ready", "hid_done", "gelu_done", "h_hi", "h_lo"))
    y_done, x1_ready = sem("y_done"), sem("x1_ready")
    qkv_done, v_evac, rope_step = sem("qkv_done"), sem("v_evac"), sem("rope_step")
    part0, res_ready, part1, part2 = (sem(n) for n in ("part0", "res_ready", "part1", "part2"))
    stored = [sem(f"stored{n}") for n in range(4)]
    dve_passed, pool_passed = sem("a_dve_passed"), sem("a_pool_passed")

    w_loaded = [sem(f"w_loaded{n}") for n in range(len(weights))]
    w_hi, w_lo, small_loaded, consts, hb2_ready = (
        sem(n) for n in ("w_hi", "w_lo", "small_loaded", "consts", "hb2_ready"))

    block = ctx.enter_context(nc.Block())

    x_v = x.rearrange("(n a p) d -> n p a d", a=TT, p=P)

    @block.sync
    def _(sp):
        def load(t):
            wait(sp, xn_ready[0], TT * t)
            wait(sp, base_ready, TT * t)
            sp.dma_start(x_in[:], x_v[bass.ds(t, 1)].rearrange("o p a d -> (o p) a d")).then_inc(x_loaded, 16)

        def store(s):
            for i in range(4):
                dst = (q_parts_d, k_parts_d)[i // 2].rearrange("b n (c j) q -> b j c n q", j=4)
                sp.wait_ge(part2, 4 * s + i + 1)
                for jj in range(2):
                    d = dst[bass.ds(s // CPB, 1), 2 * (i % 2) + jj, :, :, bass.ds((s % CPB) * CH, CH)]
                    sp.dma_start(d.rearrange("o c n q -> (o c) n q"),
                                 parts[64 * jj:64 * jj + 64, i]).then_inc(stored[i], 16)
        for i in range(4):
            sp.sem_inc(stored[i], 32)
        load(0)
        for n, (src, _, _, _) in enumerate(weights):
            sp.dma_start(stage[n][:], src.rearrange("(k p) n -> p k n", p=P)).then_inc(w_loaded[n], 16)
            if n == 0:
                for dst, src in small:
                    sp.dma_start(dst, src).then_inc(small_loaded, 16)
        load(1)
        with sp.Fori(1, NCH - 1) as t:
            load(t + 1)
            store(t - 1)
        store(NCH - 2)
        store(NCH - 1)
        for i in range(4):
            sp.wait_ge(stored[i], 32 * (NCH + 1))

    @block.gpsimd
    def _(pool):
        def rstd_of(n, t):
            hold(pool, mean_ready[n], TT * (t + 1), pool_passed)
            nc.gpsimd.tensor_scalar(rstd[:, n], mv[:, n, :, 1], EPS, None, ALU.add).then_inc(ve_ready[n], 1)
            pool.wait_ge(ve_ready[n], t + 1)
            nc.gpsimd.tensor_tensor(rstd[:, n], rstd[:, n], neg_half[:], ALU.pow).then_inc(rstd_ready[n], 1)

        def residual_base(t):
            hold(pool, x_loaded, 16 * (t + 1), pool_passed)
            for a in range(TT):
                nc.gpsimd.tensor_tensor(x1[:, bass.ds(TT * t + a, 1), :].rearrange("p o d -> p (o d)"),
                                        x_in[:, a], hb2[:], ALU.add).then_inc(base_ready, 1)

        nc.gpsimd.memset(ident[:], 0.0).then_inc(consts, 1)
        nc.gpsimd.memset(neg_half[:], -0.5).then_inc(consts, 1)
        pool.wait_ge(consts, 2)
        nc.gpsimd.affine_select(out=ident[:], in_=ident[:], compare_op=ALU.not_equal, fill=1.0,
                                base=0, pattern=[[-1, P]], channel_multiplier=1).then_inc(consts, 1)
        rstd_of(0, 0)
        pool.wait_ge(hb2_ready, 1)
        residual_base(0)
        rstd_of(0, 1)
        residual_base(1)
        rstd_of(1, 0)
        with pool.Fori(1, NCH - 1) as t:
            rstd_of(0, t + 1)
            residual_base(t + 1)
            rstd_of(1, t)
        rstd_of(1, NCH - 1)

    @block.scalar
    def _(act):
        def hidden(t, m):
            act.wait_ge(hid_done, MT * t + m + 1)
            wait(act, h_lo, MT * t + m + 1 - NGB)
            nc.scalar.activation(g[:, m % NGB], hid_ps[:, m % 2], ACT.Gelu, bias=b1_sb[:, m:m + 1]).then_inc(gelu_done, 1)

        def upper(t, m):
            act.wait_ge(gelu_done, MT * t + m + 1)
            nc.scalar.activation(h[:, 0, m], g[:, m % NGB], ACT.Copy).then_inc(h_hi, 1)

        def gelus(t, ms):
            for m in ms:
                hidden(t, m)
                if m > ms[0]:
                    upper(t, m - 1)
            upper(t, ms[-1])

        def xt_upper(n, t):
            for k in range(KT):
                act.wait_ge(xt_ps_ready[n], KT * t + k + 1)
                nc.scalar.activation(xt[n][:, 0, k], tr_ps[:, k], ACT.Copy).then_inc(xt_hi[n], 1)

        def qkv_parts(s):
            for i in range(4):
                act.wait_ge(stored[i], 32 * (s + 1))
                if i % 2 == 0:
                    act.wait_ge(qkv_done, 6 * s + i + 1)
                    src = qkv_ps[:, i % 2]
                else:
                    act.wait_ge(rope_step, 8 * s + 4 * (i // 2) + 4)
                    src = rot[:]
                nc.scalar.activation(parts[:, i, 0], src, ACT.Copy).then_inc(part0, 1)
                act.wait_ge(res_ready, 4 * s + i + 1)
                nc.scalar.activation(parts[:, i, 1], res[:, i % 2], ACT.Copy).then_inc(part1, 1)
            for n in range(2):
                act.wait_ge(qkv_done, 6 * s + 5 + n)
                dst = v_all[:, bass.ds(s // CPB, 1), :, bass.ds(s % CPB, 1), 2 * n:2 * n + 2, :]
                nc.scalar.activation(dst.rearrange("p o g e a c -> p (o g) (e a) c"),
                                     qkv_ps[:, n].rearrange("p (a g c) -> p g a c", a=2, g=HG),
                                     ACT.Copy).then_inc(v_evac, 1)

        def body(t, first=False, last=False):
            gelus(t, range(0, MT // 2))
            if not first:
                xt_upper(1, t - 1)
            gelus(t, range(MT // 2, MT))
            if not last:
                xt_upper(0, t + 1)
            if not first:
                qkv_parts(t - 1)

        def weight_upper(n):
            act.wait_ge(w_loaded[n], 16)
            nc.scalar.activation(weights[n][1][:, 0], stage[n][:], ACT.Copy).then_inc(w_hi, 1)

        act.sem_inc(v_evac, 2)
        act.wait_ge(small_loaded, 16 * len(small))
        nc.scalar.activation(hb2[:], hb2[:], ACT.Copy, scale=0.5).then_inc(hb2_ready, 1)
        weight_upper(0)
        xt_upper(0, 0)
        for n in range(1, len(weights)):
            weight_upper(n)
        act.wait_ge(w_lo, 2)
        body(0, first=True)
        with act.Fori(1, NCH - 1) as t:
            body(t)
        body(NCH - 1, last=True)
        xt_upper(1, NCH - 1)
        qkv_parts(NCH - 1)

    @block.vector
    def _(dve):
        def src_of(n, t, a):
            return x_in[:, a] if n == 0 else x1[:, bass.ds(TT * t + a, 1), :].rearrange("p o d -> p (o d)")

        def ln_stats(n, t):
            hold(dve, xn_ready[n], TT * t, dve_passed)
            if n:
                hold(dve, x1_ready, TT * (t + 1), dve_passed)
            else:
                hold(dve, x_loaded, 16 * (t + 1), dve_passed)
            for a in range(TT):
                nc.vector.bn_stats(stats[:, n, a], src_of(n, t, a)).then_inc(stats_done[n], 1)
            for a in range(TT):
                hold(dve, stats_done[n], TT * t + a + 1, dve_passed)
                nc.vector.bn_aggr(mv[:, n, a], stats[:, n, a]).then_inc(mean_ready[n], 1)

        def ln_apply(n, t):
            if n == 0:
                wait(dve, xt_ps_ready[1], KT * (t - 1))
            else:
                dve.wait_ge(xt_ps_ready[0], KT * (t + 2) if not isinstance(t, int) else KT * min(t + 2, NCH))
            dve.wait_ge(rstd_ready[n], t + 1)
            for a in range(TT):
                nc.vector.tensor_scalar(xn[:, a], src_of(n, t, a), mv[:, n, a, 0:1], rstd[:, n, a:a + 1],
                                        ALU.subtract, ALU.mult).then_inc(xn_ready[n], 1)

        def h_lower(t, ms):
            for m in ms:
                dve.wait_ge(h_hi, MT * t + m + 1)
                nc.vector.tensor_tensor(h[:, 1, m], g[:, m % NGB], h[:, 0, m].bitcast(F32),
                                        ALU.subtract).then_inc(h_lo, 1)

        def xt_lower(n, t):
            for k in range(KT):
                dve.wait_ge(xt_hi[n], KT * t + k + 1)
                nc.vector.tensor_tensor(xt[n][:, 1, k], tr_ps[:, k], xt[n][:, 0, k].bitcast(F32),
                                        ALU.subtract).then_inc(xt_lo[n], 1)

        def part_two(s, i):
            dve.wait_ge(part1, 4 * s + i + 1)
            nc.vector.tensor_tensor(parts[:, i, 2], res[:, i % 2], parts[:, i, 1],
                                    ALU.subtract).then_inc(part2, 1)

        def qkv_parts(s):
            for i in range(4):
                if i % 2:
                    dve.wait_ge(qkv_done, 6 * s + i + 1)
                    at = bass.ds((s % CPB) * CH, CH)
                    step = 8 * s + 4 * (i // 2)
                    if i == 3:
                        dve.wait_ge(part2, 4 * s + 2)
                    nc.vector.tensor_tensor(rot[:], qkv_ps[:, 1], cos_sb[:, at], ALU.mult).then_inc(rope_step, 1)
                    nc.vector.tensor_tensor(res[0:64, 1], qkv_ps[64:128, 1], sin_sb[64:128, at], ALU.mult).then_inc(rope_step, 1)
                    nc.vector.tensor_tensor(res[64:128, 1], qkv_ps[0:64, 1], sin_sb[0:64, at], ALU.mult).then_inc(rope_step, 1)
                    dve.wait_ge(rope_step, step + 3)
                    nc.vector.tensor_tensor(rot[:], rot[:], res[:, 1], ALU.add).then_inc(rope_step, 1)
                dve.wait_ge(part0, 4 * s + i + 1)
                src = rot[:] if i % 2 else qkv_ps[:, 0]
                if i >= 2:
                    dve.wait_ge(part2, 4 * s + i - 1)
                nc.vector.tensor_tensor(res[:, i % 2], src, parts[:, i, 0], ALU.subtract).then_inc(res_ready, 1)
                if i:
                    part_two(s, i - 1)
            part_two(s, 3)
            dve.wait_ge(part2, 4 * s + 4)

        def residual(t):
            dve.wait_ge(base_ready, TT * (t + 1))
            for a in range(TT):
                dve.wait_ge(y_done, TT * t + 2 * (a // 2) + 2)
                place = x1[:, bass.ds(TT * t + a, 1), :].rearrange("p o d -> p (o d)")
                nc.vector.scalar_tensor_tensor(place, y_ps[:, a // 2, (a % 2) * D:(a % 2 + 1) * D], 0.5, place,
                                               ALU.mult, ALU.add).then_inc(x1_ready, 1)

        def body(t, first=False, last=False):
            h_lower(t, range(0, MT // 2))
            if not last:
                ln_stats(0, t + 1)
            if not first:
                xt_lower(1, t - 1)
            if not last:
                ln_apply(0, t + 1)
            h_lower(t, range(MT // 2, MT))
            if not last:
                xt_lower(0, t + 1)
            if not first:
                qkv_parts(t - 1)
            residual(t)
            ln_stats(1, t)
            ln_apply(1, t)

        def weight_lower(n):
            dve.wait_ge(w_hi, n + 1)
            nc.vector.tensor_tensor(weights[n][1][:, 1], stage[n][:], weights[n][1][:, 0].bitcast(F32),
                                    ALU.subtract).then_inc(w_lo, 1)

        ln_stats(0, 0)
        ln_apply(0, 0)
        weight_lower(0)
        xt_lower(0, 0)
        for n in range(1, len(weights)):
            weight_lower(n)
        dve.wait_ge(w_lo, len(weights))
        dve.wait_ge(small_loaded, 16 * len(small))
        body(0, first=True)
        with dve.Fori(1, NCH - 1) as t:
            body(t)
        body(NCH - 1, last=True)
        xt_lower(1, NCH - 1)
        qkv_parts(NCH - 1)

    @block.tensor
    def _(pe):
        def transposes(n, t):
            pe.wait_ge(xn_ready[n], TT * (t + 1))
            if n == 0:
                wait(pe, xt_lo[1], KT * (t - 1))
            else:
                wait(pe, xt_lo[0], KT * (t + 2) if not isinstance(t, int) else KT * min(t + 2, NCH))
            for k in range(KT):
                for a in range(TT):
                    last = nc.tensor.transpose(tr_ps[:, k, P * a:P * (a + 1)], xn[:, a, P * k:P * (k + 1)], ident[:])
                last.then_inc(xt_ps_ready[n], 1)

        def ffn_up(t, ms):
            pe.wait_ge(xt_lo[0], KT * (t + 1))
            for m in ms:
                wait(pe, gelu_done, MT * t + m - 1)
                for k in range(KT):
                    last = mm3(nc, hid_ps[:, m % 2], lambda p: w1[:, p, k, P * m:P * (m + 1)],
                               lambda p: xt[0][:, p, k], None, k, KT)
                last.then_inc(hid_done, 1)

        def ffn_down(t, a):
            if a == 0:
                if isinstance(t, int) and t == 0:
                    pe.wait_ge(w_lo, len(weights))
                pe.wait_ge(h_lo, MT * (t + 1))
                wait(pe, x1_ready, TT * t)
            for k in range(MT):
                last = mm3(nc, y_ps[:, a // 2, (a % 2) * D:(a % 2 + 1) * D],
                           lambda p: h[:, p, k, P * a:P * (a + 1)], lambda p: w2[:, p, k], None, k, MT)
            last.then_inc(y_done, 1)

        def qk(s, m):
            if m == 0:
                pe.wait_ge(xt_lo[1], KT * (s + 1))
            if m < 2:
                pe.wait_ge(v_evac, 2 * s + m + 1)
            else:
                pe.wait_ge(res_ready, 4 * s + m - 1)
            for k in range(KT):
                last = mm3(nc, qkv_ps[:, m % 2], lambda p: wqk[:, p, k, P * m:P * (m + 1)],
                           lambda p: xt[1][:, p, k], None, k, KT)
            last.then_inc(qkv_done, 1)

        def values(s, n):
            pe.wait_ge(res_ready, 4 * s + 3 + n)
            for a in range(2):
                for k in range(KT):
                    tile = 2 * n + a
                    last = mm3(nc, qkv_ps[:, n, a * D:(a + 1) * D],
                               lambda p: xt[1][:, p, k, P * tile:P * (tile + 1)],
                               lambda p: wv[:, p, k], None, k, KT)
            last.then_inc(qkv_done, 1)

        def body(t, first=False, last=False):
            ffn_up(t, range(0, MT // 2))
            if not first:
                transposes(1, t - 1)
            ffn_up(t, range(MT // 2, MT))
            if not last:
                transposes(0, t + 1)
            for a in range(TT):
                if not first:
                    if a == 0:
                        qk(t - 1, 0)
                        qk(t - 1, 1)
                    elif a < 3:
                        qk(t - 1, a + 1)
                    else:
                        values(t - 1, 0)
                ffn_down(t, a)
            if not first:
                values(t - 1, 1)

        pe.wait_ge(consts, 3)
        transposes(0, 0)
        pe.wait_ge(w_lo, 1)
        body(0, first=True)
        with pe.Fori(1, NCH - 1) as t:
            body(t)
        body(NCH - 1, last=True)
        transposes(1, NCH - 1)
        for m in range(4):
            qk(NCH - 1, m)
        for n in range(2):
            values(NCH - 1, n)


def phase_b(nc, ctx, sb, ps, v_all, ident, q_parts_d, k_parts_d, o_d):
    sem = lambda name: ctx.enter_context(nc.semaphore(name))
    q_st = [sb(ctx, f"q_st{n}", [P, 2, GH, CH], BF16) for n in range(RING)]
    k_st = [sb(ctx, f"k_st{n}", [P, GH, S], BF16) for n in range(RING)]
    va = [sb(ctx, f"va{n}", [P, QT, GH, VW]) for n in range(RING)]
    probs = [sb(ctx, f"probs{n}", [P, GH, CH]) for n in range(RING)]
    ident_bf = sb(ctx, "ident_bf", [P, P], BF16)
    mask_bf = sb(ctx, "mask_bf", [P, P], BF16)
    mask_t_bf = sb(ctx, "mask_t_bf", [P, P], BF16)
    nmax = [sb(ctx, f"nmax{n}", [P, GH, 4]) for n in range(2)]
    pmax = sb(ctx, "pmax", [P, GH, 4, 2])
    n_row = [sb(ctx, f"n_row{n}", [GH * 4, P]) for n in range(2)]
    n_res = [sb(ctx, f"n_res{n}", [GH * 4, P]) for n in range(2)]
    n_part = [sb(ctx, f"n_part{n}", [GH * 4, NPART, P], BF16) for n in range(2)]
    o_sb = [sb(ctx, f"o_sb{n}", [P, CH]) for n in range(2)]

    st_ps = [ps(ctx, f"st_ps{n}", [P, 2, CH]) for n in range(2)]
    s_ps = ps(ctx, "s_ps", [P, 2, CH])
    pv_ps = ps(ctx, "pv_ps", [P, 2, CH])

    loaded = [sem(f"stack_loaded{n}") for n in range(RING)]
    consts, ones_rows, va_ready = sem("b_consts"), sem("ones_rows"), sem("va_ready")
    s_done, max_done, nmax1_ready = sem("s_done"), sem("max_done"), sem("nmax1_ready")
    nt_done, n_row_ready, split_step = sem("nt_done"), sem("n_row_ready"), sem("split_step")
    m_rows = [sem(f"m_rows{n}") for n in range(2)]
    st_done, exp_done, pv_done = (sem(n) for n in ("st_done", "exp_done", "pv_done"))
    o_ready, pool_passed = sem("o_ready"), sem("b_pool_passed")
    o_stored = [sem(f"o_stored{n}") for n in range(2)]
    NCONST = 6 + RING
    PER_LOAD = 16 * 3 * NB

    qs_v = q_parts_d.rearrange("b n (e h r) q -> b n e r h q", h=GH, r=DQ)
    ks_v = k_parts_d.rearrange("b n (e h r) q -> b n e r h q", h=GH, r=DQ)
    o_v = o_d.rearrange("(g p) q -> g p q", p=P)
    v_v = v_all[:].rearrange("p b g c a w -> p (b g) (c a) w")

    block = ctx.enter_context(nc.Block())

    def groups(eng, body):
        body(0, 0)
        with eng.Fori(0, (NG - 1) // RING - 1) as i:
            for r in range(1, RING + 1):
                body(RING * i + r, r % RING)
        for g in range(NG - RING, NG):
            body(g, g % RING)

    def is_last(g):
        return isinstance(g, int) and g == NG - 1

    @block.sync
    def _(sp):
        def load(g, r):
            for n in range(NB):
                rows = slice(DQ * n, DQ * (n + 1))
                src = ks_v[bass.ds(g // HG, 1), K_BLOCKS[n], bass.ds(g % HG, 1)]
                sp.dma_start(k_st[r][rows], src.rearrange("o e r h q -> (o e r) h q")).then_inc(loaded[r], 16)
                for half in range(2):
                    src = qs_v[bass.ds(g // HG, 1), Q_BLOCKS[n], bass.ds(g % HG, 1), :, :, CH * half:CH * (half + 1)]
                    sp.dma_start(q_st[r][rows, half], src.rearrange("o e r h q -> (o e r) h q")).then_inc(loaded[r], 16)

        def max_rows(half, g, r):
            sp.wait_ge(split_step, 4 * (2 * g + half) + 4)
            for part in range(NPART):
                sp.dma_start(q_st[r][ROWS + part:ROWS + part + 1, half].rearrange("p h q -> p (h q)"),
                             n_part[half][:, part, :]).then_inc(m_rows[half], 16)

        def store(c, g):
            sp.wait_ge(o_ready, 2 * g + c + 1)
            sp.dma_start(o_v[bass.ds(g, 1), :, CH * c:CH * (c + 1)].rearrange("o p q -> (o p) q"),
                         o_sb[c][:]).then_inc(o_stored[c], 16)

        def body(g, r):
            max_rows(1, g, r)
            if not isinstance(g, int) or g + 2 < NG:
                sp.wait_ge(st_done, 2 * NU * g + 1)
                load(g + 2, (r + 2) % RING)
            if not isinstance(g, int) or g + 1 < NG:
                max_rows(0, g + 1, (r + 1) % RING)
            store(0, g)
            store(1, g)

        load(0, 0)
        load(1, 1)
        max_rows(0, 0, 0)
        groups(sp, body)
        for c in range(2):
            sp.wait_ge(o_stored[c], 16 * NG)

    @block.gpsimd
    def _(pool):
        nc.gpsimd.memset(ident_bf[:], 0.0).then_inc(consts, 1)
        nc.gpsimd.memset(mask_bf[:], 0.0).then_inc(consts, 1)
        nc.gpsimd.memset(mask_t_bf[:], 0.0).then_inc(consts, 1)
        for r in range(RING):
            nc.gpsimd.memset(va[r][:, :, :, DV:VW], 1.0).then_inc(consts, 1)
        pool.wait_ge(consts, 3)
        nc.gpsimd.affine_select(out=mask_t_bf[:], in_=mask_t_bf[:], compare_op=ALU.is_ge, fill=NEG, base=0,
                                pattern=[[1, P]], channel_multiplier=-1).then_inc(consts, 1)
        nc.gpsimd.affine_select(out=ident_bf[:], in_=ident_bf[:], compare_op=ALU.not_equal, fill=1.0, base=0,
                                pattern=[[-1, P]], channel_multiplier=1).then_inc(consts, 1)
        nc.gpsimd.affine_select(out=mask_bf[:], in_=mask_bf[:], compare_op=ALU.is_ge, fill=NEG, base=0,
                                pattern=[[-1, P]], channel_multiplier=1).then_inc(consts, 1)

        def values(g, r):
            nc.gpsimd.tensor_copy(va[r][:, :, :, 0:DV],
                                  v_v[:, bass.ds(g, 1), :, :].rearrange("p o j (h d) -> p (o j) h d", h=GH)
                                  ).then_inc(va_ready, 1)

        def split(half, g):
            k = 2 * g + half
            hold(pool, n_row_ready, k + 1, pool_passed)
            nc.gpsimd.tensor_copy(n_part[half][:, 0], n_row[half][:]).then_inc(split_step, 1)
            pool.wait_ge(split_step, 4 * k + 1)
            nc.gpsimd.tensor_tensor(n_res[half][:], n_row[half][:], n_part[half][:, 0], ALU.subtract).then_inc(split_step, 1)
            hold(pool, split_step, 4 * k + 2, pool_passed)
            nc.gpsimd.tensor_copy(n_part[half][:, 1], n_res[half][:]).then_inc(split_step, 1)
            pool.wait_ge(split_step, 4 * k + 3)
            nc.gpsimd.tensor_tensor(n_part[half][:, 2], n_res[half][:], n_part[half][:, 1], ALU.subtract).then_inc(split_step, 1)

        def body(g, r):
            split(1, g)
            if not is_last(g):
                values(g + 1, (r + 1) % RING)
                split(0, g + 1)

        values(0, 0)
        split(0, 0)
        groups(pool, body)

    @block.vector
    def _(dve):
        for r in range(RING):
            nc.vector.memset(k_st[r][ROWS:ROWS_M], 1.0).then_inc(ones_rows, 1)

        def maxima(g, k):
            i, part, heads, _, w = ITEMS[k]
            dve.wait_ge(s_done, NI * g + k + 1)
            slot = (1 + STREAM[1:].index(("S", k))) % 2
            src = s_ps[:, slot, 0:w * len(heads)].rearrange("p (h k) -> p h k", k=w)
            h0, h1 = heads[0], heads[-1] + 1
            if i < 4:
                nc.vector.tensor_reduce(nmax[0][:, h0:h1, i], src, axis=AX.X, op=ALU.max, negate=True).then_inc(max_done, 1)
            else:
                nc.vector.tensor_reduce(pmax[:, h0:h1, i - 4, part], src, axis=AX.X, op=ALU.max).then_inc(max_done, 1)

        def all_maxima(g):
            for k in range(NI):
                maxima(g, k)
            dve.wait_ge(max_done, NI * (g + 1))
            nc.vector.tensor_reduce(nmax[1][:], pmax[:], axis=AX.X, op=ALU.max, negate=True).then_inc(nmax1_ready, 1)

        def body(g, r):
            if not is_last(g):
                all_maxima(g + 1)

        all_maxima(0)
        groups(dve, body)

    @block.scalar
    def _(act):
        def row(half, g):
            k = 2 * g + half
            x = STREAM.index((f"T{half}", 0))
            act.wait_ge(nt_done, k + 1)
            nc.scalar.activation(n_row[half][:], s_ps[0:GH * 4, x % 2, 0:P], ACT.Copy).then_inc(n_row_ready, 1)

        def exps(g, u):
            _, w = unit_span(*UNITS[u])
            for hp in range(2):
                act.wait_ge(st_done, 2 * (NU * g + u) + hp + 1)
                if hp == 0:
                    wait(act, pv_done, NU * g + u - RING + 1)
                nc.scalar.activation(probs[u % RING][:, 2 * hp:2 * hp + 2, 0:w], st_ps[hp][:, :, 0:w], ACT.Exp,
                                     scale=SCALE).then_inc(exp_done, 1)

        def evacuate(c, g):
            last_unit = 3 if c == 0 else NU - 1
            act.wait_ge(pv_done, NU * g + last_unit + 1)
            wait(act, o_stored[c], 16 * g)
            nc.scalar.activation(o_sb[c][:], pv_ps[:, c], ACT.Copy).then_inc(o_ready, 1)

        def body(g, r):
            for u in range(NU):
                exps(g, u)
                if u == T_UNIT[1]:
                    row(1, g)
                if u == T_UNIT[0] and not is_last(g):
                    row(0, g + 1)
                if u == 5:
                    evacuate(0, g)
                if u == 1 and not (isinstance(g, int) and g == 0):
                    evacuate(1, g - 1)
            if is_last(g):
                evacuate(1, g)

        row(0, 0)
        groups(act, body)

    @block.tensor
    def _(pe):
        def slot_free(g, x):
            y = x - 2
            g, y = (g, y) if y >= 0 else (g - 1, y + NS)
            kind, k = STREAM[y]
            if isinstance(g, int) and (g < 0 or (g == 0 and y == 0)):
                return
            if kind == "S":
                pe.wait_ge(max_done, NI * g + k + 1)
            elif kind == "T0":
                pe.wait_ge(n_row_ready, 2 * g + 1)
            else:
                pe.wait_ge(n_row_ready, 2 * (g - 1) + 2)

        def stream(g, x, r):
            kind, k = STREAM[x]
            slot_free(g, x)
            if kind == "S":
                _, _, heads, k0, w = ITEMS[k]
                i = ITEMS[k][0]
                for n, hd in enumerate(heads):
                    o = s_ps[:, x % 2, n * w:(n + 1) * w]
                    diagonal = k0 + w == P * (i + 1)
                    last = nc.tensor.matmul(o, q_st[r][0:ROWS, i // 4, hd, P * (i % 4):P * (i % 4 + 1)],
                                            k_st[r][0:ROWS, hd, k0:k0 + w], start=True, stop=not diagonal)
                    if diagonal:
                        last = nc.tensor.matmul(o[:, w - P:w], ident_bf[:], mask_bf[:], start=False, stop=True)
                last.then_inc(s_done, 1)
                return
            if kind == "T0":
                pe.wait_ge(max_done, NI * g + FIRST_HALF)
            else:
                pe.wait_ge(nmax1_ready, g)
            nc.tensor.matmul(s_ps[0:GH * 4, x % 2, 0:P], nmax[int(kind[1])][:].rearrange("p h t -> p (h t)"),
                             ident[:], start=True, stop=True).then_inc(nt_done, 1)

        def scores(g, u, hp, r):
            c, j = UNITS[u]
            q0, w = unit_span(c, j)
            if j == 0 and hp == 0:
                pe.wait_ge(m_rows[c], 16 * NPART * (g + 1))
            wait(pe, exp_done, 2 * (NU * g + u) + hp - 1)
            for n in range(2):
                hd = 2 * hp + n
                last = nc.tensor.matmul(st_ps[hp][:, n, 0:w], k_st[r][0:ROWS_M, hd, P * j:P * (j + 1)],
                                        q_st[r][0:ROWS_M, c, hd, q0 - CH * c:q0 - CH * c + w],
                                        start=True, stop=u not in DIAG)
                if u in DIAG:
                    last = nc.tensor.matmul(st_ps[hp][:, n, 0:P], ident_bf[:], mask_t_bf[:], start=False, stop=True)
            last.then_inc(st_done, 1)

        def sums(g, u, r):
            c, j = UNITS[u]
            q0, w = unit_span(c, j)
            pe.wait_ge(exp_done, 2 * (NU * g + u) + 2)
            if j == 0:
                wait(pe, o_ready, 2 * g + c - 1)
                if c == 0:
                    pe.wait_ge(va_ready, g + 1)
            for hd in range(GH):
                last = nc.tensor.matmul(pv_ps[VW * hd:VW * (hd + 1), c, q0 - CH * c:q0 - CH * c + w],
                                        va[r][:, j, hd, :], probs[u % RING][:, hd, 0:w],
                                        start=j == 0, stop=j == 4 * (c + 1) - 1)
            last.then_inc(pv_done, 1)

        def body(g, r):
            nxt = (r + 1) % RING

            def stream_step(u, n):
                run = range(u * NS // NU, (u + 1) * NS // NU)
                for x in run[n:n + 1] if n < 2 else run[2:]:
                    if x == 1 and not is_last(g):
                        pe.wait_ge(loaded[nxt], PER_LOAD * ((g + 1) // RING + 1))
                    if not is_last(g) or x == 0:
                        stream(g + 1, x, nxt)

            for u in range(NU):
                scores(g, u, 0, r)
                stream_step(u, 0)
                scores(g, u, 1, r)
                stream_step(u, 1)
                if u:
                    sums(g, u - 1, r)
                elif not (isinstance(g, int) and g == 0):
                    sums(g - 1, NU - 1, (r - 1) % RING)
                stream_step(u, 2)
            if is_last(g):
                sums(g, NU - 1, r)

        pe.wait_ge(consts, NCONST)
        pe.wait_ge(ones_rows, RING)
        pe.wait_ge(loaded[0], PER_LOAD)
        for x in range(1, NS):
            stream(0, x, 0)
        groups(pe, body)


T_UNIT = {n: next(u for u in range(NU) if u * NS // NU <= STREAM.index((f"T{n}", 0)) < (u + 1) * NS // NU)
          for n in range(2)}


def phase_c(nc, ctx, sb, ps, x1, w1, w2, wo, b1_sb, hb2, ident, neg_half, o_d, out):
    sem = lambda name: ctx.enter_context(nc.semaphore(name))
    num = sb(ctx, "num", [P, KT, CH])
    den = sb(ctx, "den", [P, KT, CH])
    rden = sb(ctx, "rden", [P, KT, CH])
    att = sb(ctx, "att", [P, KT, CH])
    att_p = sb(ctx, "att_p", [P, 2, KT, CH], F32R)
    stats = sb(ctx, "c_stats", [P, TT, 6])
    mv = sb(ctx, "c_mv", [P, TT, 2])
    ve = sb(ctx, "c_ve", [P, TT])
    rstd = sb(ctx, "c_rstd", [P, TT])
    xn = sb(ctx, "c_xn", [P, TT, D])
    xt = sb(ctx, "c_xt", [P, 2, KT, CH], F32R)
    NGB = 4
    g = sb(ctx, "c_g", [P, NGB, CH])
    h = sb(ctx, "c_h", [P, 2, MT, CH], F32R)
    y = sb(ctx, "c_y", [P, TT, D])

    hid_ps = ps(ctx, "c_hid_ps", [P, 2, CH])
    y_ps = ps(ctx, "c_y_ps", [P, 2, CH])
    tr_ps = ps(ctx, "c_tr_ps", [P, KT, CH])
    wo_ps = ps(ctx, "c_wo_ps", [P, 2, CH])

    o_loaded, rden_ready, att_ready, att_hi, att_lo, wo_done, x2_ready = (
        sem(n) for n in ("o_loaded", "rden_ready", "att_ready", "att_hi", "att_lo", "wo_done", "x2_ready"))
    stats_done, mean_ready, ve_ready, rstd_ready, xn_ready = (
        sem(n) for n in ("c_stats_done", "c_mean_ready", "c_ve_ready", "c_rstd_ready", "c_xn_ready"))
    xt_ps_ready, xt_hi, xt_lo, base_ready = (sem(n) for n in ("c_xt_ps_ready", "c_xt_hi", "c_xt_lo", "c_base_ready"))
    hid_done, gelu_done, h_hi, h_lo = (sem(n) for n in ("c_hid_done", "c_gelu_done", "c_h_hi", "c_h_lo"))
    y_done, y_ready, y_stored = sem("c_y_done"), sem("c_y_ready"), sem("c_y_stored")
    dve_passed, pool_passed = sem("c_dve_passed"), sem("c_pool_passed")

    o_v = o_d.rearrange("(b k e s r) q -> b k s e r q", b=B, k=KT, s=2, r=DV)
    out_v = out.rearrange("(n a p) d -> n p a d", a=TT, p=P)

    block = ctx.enter_context(nc.Block())

    @block.sync
    def _(sp):
        def load(t):
            wait(sp, att_ready, t)
            for k in range(KT):
                for s, dst in ((0, num), (1, den)):
                    src = o_v[bass.ds(t // CPB, 1), k, s, :, :, bass.ds((t % CPB) * CH, CH)]
                    sp.dma_start(dst[:, k, :], src.rearrange("o e r q -> (o e) r q")).then_inc(o_loaded, 16)

        def store(t):
            sp.wait_ge(y_ready, TT * (t + 1))
            sp.dma_start(out_v[bass.ds(t, 1)].rearrange("o p a d -> (o p) a d"), y[:]).then_inc(y_stored, 16)

        load(0)
        load(1)
        load(2)
        store(0)
        with sp.Fori(1, NCH - 2) as t:
            load(t + 2)
            store(t)
        store(NCH - 2)
        store(NCH - 1)
        sp.wait_ge(y_stored, 16 * NCH)

    @block.gpsimd
    def _(pool):
        def norm(t):
            hold(pool, mean_ready, TT * (t + 1), pool_passed)
            nc.gpsimd.tensor_scalar(ve[:], mv[:, :, 1], EPS, None, ALU.add).then_inc(ve_ready, 1)
            pool.wait_ge(ve_ready, t + 1)
            nc.gpsimd.tensor_tensor(rstd[:], ve[:], neg_half[:], ALU.pow).then_inc(rstd_ready, 1)

        def residual_base(t):
            hold(pool, xn_ready, TT * (t + 1), pool_passed)
            for a in range(TT):
                place = x1[:, bass.ds(TT * t + a, 1), :].rearrange("p o d -> p (o d)")
                nc.gpsimd.tensor_tensor(place, place, hb2[:], ALU.add).then_inc(base_ready, 1)

        norm(0)
        residual_base(0)
        norm(1)
        residual_base(1)
        with pool.Fori(1, NCH - 1) as t:
            norm(t + 1)
            residual_base(t + 1)

    @block.scalar
    def _(act):
        def hidden(t, m):
            act.wait_ge(hid_done, MT * t + m + 1)
            wait(act, h_lo, MT * t + m + 1 - NGB)
            nc.scalar.activation(g[:, m % NGB], hid_ps[:, m % 2], ACT.Gelu, bias=b1_sb[:, m:m + 1]).then_inc(gelu_done, 1)

        def upper(t, m):
            act.wait_ge(gelu_done, MT * t + m + 1)
            nc.scalar.activation(h[:, 0, m], g[:, m % NGB], ACT.Copy).then_inc(h_hi, 1)

        def gelus(t, ms):
            for m in ms:
                hidden(t, m)
                if m > ms[0]:
                    upper(t, m - 1)
            upper(t, ms[-1])

        def xt_upper(t):
            for k in range(KT):
                act.wait_ge(xt_ps_ready, KT * t + k + 1)
                nc.scalar.activation(xt[:, 0, k], tr_ps[:, k], ACT.Copy).then_inc(xt_hi, 1)

        def att_upper(t):
            act.wait_ge(att_ready, t + 1)
            wait(act, wo_done, TT * t)
            nc.scalar.activation(att_p[:, 0], att[:], ACT.Copy).then_inc(att_hi, 1)

        def body(t, nxt=True, second=True):
            gelus(t, range(MT // 2))
            gelus(t, range(MT // 2, MT))
            if nxt:
                xt_upper(t + 1)
            if second:
                att_upper(t + 2)

        att_upper(0)
        xt_upper(0)
        att_upper(1)
        body(0)
        with act.Fori(1, NCH - 2) as t:
            body(t)
        body(NCH - 2, second=False)
        body(NCH - 1, nxt=False, second=False)

    @block.vector
    def _(dve):
        def x1_tile(t, a):
            return x1[:, bass.ds(TT * t + a, 1), :].rearrange("p o d -> p (o d)")

        def attention_rows(t):
            dve.wait_ge(o_loaded, 64 * (t + 1))
            wait(dve, att_lo, t)
            for k in range(KT):
                nc.vector.reciprocal(rden[:, k], den[:, k]).then_inc(rden_ready, 1)
            dve.wait_ge(rden_ready, KT * (t + 1))
            nc.vector.tensor_tensor(att[:], num[:], rden[:], ALU.mult).then_inc(att_ready, 1)

        def att_lower(t):
            dve.wait_ge(att_hi, t + 1)
            nc.vector.tensor_tensor(att_p[:, 1], att[:], att_p[:, 0].bitcast(F32), ALU.subtract).then_inc(att_lo, 1)

        def residual_attention(t):
            for a in range(TT):
                dve.wait_ge(wo_done, TT * t + 2 * (a // 2) + 2)
                nc.vector.tensor_tensor(x1_tile(t, a), wo_ps[:, a // 2, (a % 2) * D:(a % 2 + 1) * D],
                                        x1_tile(t, a), ALU.add).then_inc(x2_ready, 1)

        def layernorm(t):
            hold(dve, xn_ready, TT * t, dve_passed)
            for a in range(TT):
                hold(dve, x2_ready, TT * t + a + 1, dve_passed)
                nc.vector.bn_stats(stats[:, a], x1_tile(t, a)).then_inc(stats_done, 1)
            for a in range(TT):
                hold(dve, stats_done, TT * t + a + 1, dve_passed)
                nc.vector.bn_aggr(mv[:, a], stats[:, a]).then_inc(mean_ready, 1)
            dve.wait_ge(rstd_ready, t + 1)
            wait(dve, xt_ps_ready, KT * t)
            for a in range(TT):
                nc.vector.tensor_scalar(xn[:, a], x1_tile(t, a), mv[:, a, 0:1], rstd[:, a:a + 1],
                                        ALU.subtract, ALU.mult).then_inc(xn_ready, 1)

        def h_lower(t, ms):
            for m in ms:
                dve.wait_ge(h_hi, MT * t + m + 1)
                nc.vector.tensor_tensor(h[:, 1, m], g[:, m % NGB], h[:, 0, m].bitcast(F32),
                                        ALU.subtract).then_inc(h_lo, 1)

        def xt_lower(t):
            for k in range(KT):
                dve.wait_ge(xt_hi, KT * t + k + 1)
                nc.vector.tensor_tensor(xt[:, 1, k], tr_ps[:, k], xt[:, 0, k].bitcast(F32),
                                        ALU.subtract).then_inc(xt_lo, 1)

        def residual(t):
            dve.wait_ge(base_ready, TT * (t + 1))
            wait(dve, y_stored, 16 * t)
            for a in range(TT):
                dve.wait_ge(y_done, TT * t + 2 * (a // 2) + 2)
                nc.vector.scalar_tensor_tensor(y[:, a], y_ps[:, a // 2, (a % 2) * D:(a % 2 + 1) * D], 0.5,
                                               x1_tile(t, a), ALU.mult, ALU.add).then_inc(y_ready, 1)

        def body(t, nxt=True, second=True):
            h_lower(t, range(MT // 2))
            if nxt:
                residual_attention(t + 1)
                layernorm(t + 1)
            h_lower(t, range(MT // 2, MT))
            if nxt:
                xt_lower(t + 1)
            if second:
                attention_rows(t + 2)
                att_lower(t + 2)
            residual(t)

        attention_rows(0)
        att_lower(0)
        residual_attention(0)
        layernorm(0)
        xt_lower(0)
        attention_rows(1)
        att_lower(1)
        body(0)
        with dve.Fori(1, NCH - 2) as t:
            body(t)
        body(NCH - 2, second=False)
        body(NCH - 1, nxt=False, second=False)

    @block.tensor
    def _(pe):
        def project(t):
            pe.wait_ge(att_lo, t + 1)
            wait(pe, x2_ready, TT * t)
            for a in range(TT):
                for k in range(KT):
                    last = mm3(nc, wo_ps[:, a // 2, (a % 2) * D:(a % 2 + 1) * D],
                               lambda p: att_p[:, p, k, P * a:P * (a + 1)], lambda p: wo[:, p, k], None, k, KT)
                last.then_inc(wo_done, 1)

        def transposes(t):
            pe.wait_ge(xn_ready, TT * (t + 1))
            for k in range(KT):
                for a in range(TT):
                    last = nc.tensor.transpose(tr_ps[:, k, P * a:P * (a + 1)], xn[:, a, P * k:P * (k + 1)], ident[:])
                last.then_inc(xt_ps_ready, 1)

        def ffn_up(t, ms):
            pe.wait_ge(xt_lo, KT * (t + 1))
            for m in ms:
                wait(pe, gelu_done, MT * t + m - 1)
                for k in range(KT):
                    last = mm3(nc, hid_ps[:, m % 2], lambda p: w1[:, p, k, P * m:P * (m + 1)],
                               lambda p: xt[:, p, k], None, k, KT)
                last.then_inc(hid_done, 1)

        def ffn_down(t):
            pe.wait_ge(h_lo, MT * (t + 1))
            wait(pe, y_ready, TT * t)
            for a in range(TT):
                for k in range(MT):
                    last = mm3(nc, y_ps[:, a // 2, (a % 2) * D:(a % 2 + 1) * D],
                               lambda p: h[:, p, k, P * a:P * (a + 1)], lambda p: w2[:, p, k], None, k, MT)
                last.then_inc(y_done, 1)

        def body(t, nxt=True):
            ffn_up(t, range(MT // 2))
            if nxt:
                project(t + 1)
            ffn_up(t, range(MT // 2, MT))
            if nxt:
                transposes(t + 1)
            ffn_down(t)

        project(0)
        transposes(0)
        body(0)
        with pe.Fori(1, NCH - 1) as t:
            body(t)
        body(NCH - 1, nxt=False)



def rope_tables():
    inv_freq = (np.float32(1.0) / np.float32(10000.0) ** (np.arange(0, 8, 2, dtype=np.float32) / np.float32(8)))
    ang = np.arange(S, dtype=np.float32)[None, :] * inv_freq.astype(np.float32)[:, None]
    rows = np.arange(P) % 4
    sign = np.where(np.arange(P) < P // 2, 1.0, -1.0).astype(np.float32)
    return np.cos(ang)[rows], np.sin(ang)[rows] * sign[:, None]


def kernel(**inputs):
    import concourse.bacc as bacc
    from concourse.bass_utils import run_bass_kernel_spmd

    a = {k[3:]: np.asarray(v) for k, v in inputs.items()}

    def rows(w):
        return w.reshape(H, 2, 4, D).transpose(1, 0, 2, 3).reshape(P, D)

    wqk = np.concatenate([rows(a[n]) for n in ("attn_Wq_sem", "attn_Wq_geo", "attn_Wk_sem", "attn_Wk_geo")])
    cos, sin = rope_tables()
    arrays = {
        "x": a["attn_x"].reshape(B * S, D),
        "w1t": a["ffn_proj1"].T, "w2t": a["ffn_proj2"].T, "wqkt": wqk.T, "wvt": a["attn_Wv"].T,
        "wot": a["attn_Wo"].T, "b1": a["ffn_proj1_bias"].reshape(MT, P).T, "b2": a["ffn_proj2_bias"],
        "cos": cos, "sin": sin,
    }
    arrays = {f"in_{k}": np.ascontiguousarray(v) for k, v in arrays.items()}
    nc = bacc.Bacc("TRN2", target_bir_lowering=False, num_devices=1)
    args = [nc.dram_tensor(k, v.shape, mybir.dt.from_np(v.dtype), kind="ExternalInput").ap() for k, v in arrays.items()]
    args.append(nc.dram_tensor("out_0", (B * S, D), F32, kind="ExternalOutput").ap())
    macaron(nc, *args)
    r = run_bass_kernel_spmd(nc, [arrays], core_ids=[0])
    return r.results[0]["out_0"].reshape(B, S, D)
```

```python
from contextlib import ExitStack

import numpy as np

import concourse.bass as bass
from concourse import mybir

F32 = mybir.dt.float32
F32R = mybir.dt.float32r
BF16 = mybir.dt.bfloat16
ALU = mybir.AluOpType
ACT = mybir.ActivationFunctionType
AX = mybir.AxisListType

P = 128
B, S, D, HID, H = 4, 1024, 256, 1024, 16
DQ, DV = 16, 16
CH = 512
NCH = B * S // CH
CPB = S // CH
TT = CH // P
KT = D // P
MT = HID // P
GH = 4
HG = H // GH
NG = B * HG
QT = S // P
NPART = 3
Q_BLOCKS = (0, 0, 1, 1, 0, 2)
K_BLOCKS = (0, 1, 0, 1, 2, 0)
NB = len(Q_BLOCKS)
ROWS = NB * DQ
ROWS_M = ROWS + NPART
VW = 32
EPS = 1e-5
SCALE = 0.25
NEG = -3.0e38
RING = 3
PASSES = ((0, 0), (1, 0), (0, 1))

UNITS = [(c, j) for c in range(2) for j in range(4 * (c + 1))]
NU = len(UNITS)


def unit_span(c, j):
    q0 = max(CH * c, P * j)
    return q0, CH * (c + 1) - q0


DIAG = [u for u, (c, j) in enumerate(UNITS) if unit_span(c, j)[0] == P * j]


def score_items():
    items = []
    for i in range(QT):
        for part, k0 in enumerate(range(0, P * (i + 1), CH)):
            w = min(CH, P * (i + 1) - k0)
            per = min(GH, CH // w)
            items += [(i, part, tuple(range(h, h + per)), k0, w) for h in range(0, GH, per)]
    return items


ITEMS = score_items()
NI = len(ITEMS)
FIRST_HALF = sum(i < 4 for i, *_ in ITEMS)
STREAM = [("S", k) for k in range(NI)]
STREAM.insert(FIRST_HALF + 4, ("T0", 0))
STREAM.insert(3, ("T1", 0))
NS = len(STREAM)
BANKS = 3
assert NS % BANKS == RING % BANKS + 1


def spread_stream():
    widths = [unit_span(*unit)[1] for unit in UNITS]
    columns = []
    for u, w in enumerate(widths):
        masks = 2 * P if u in DIAG else 0
        columns += [2 * w + masks, 2 * w + masks, 5 * widths[u - 1]]
    total, done, steps, x = sum(columns), 0, [], 0
    for c in columns:
        done += c
        end = max(x, round(NS * done / total))
        steps.append(range(x, end))
        x = end
    assert x == NS
    return steps


STEPS = spread_stream()


class Programs:

    def __init__(self, sync, gpsimd, scalar, vector, tensor, **signals):
        self.sync, self.gpsimd, self.scalar, self.vector, self.tensor = sync, gpsimd, scalar, vector, tensor
        self.signals = signals


def wait(eng, sem, value):
    if not isinstance(value, int) or value > 0:
        eng.wait_ge(sem, value)


def hold(eng, sem, value, passed):
    if not isinstance(value, int) or value > 0:
        eng.wait_ge(sem, value)
        eng.sem_inc(passed, 1)


def macaron(nc, x, w1t, w2t, wqkt, wvt, wot, b1, b2, cos, sin, out):
    ctx = ExitStack()
    with ctx:
        sem = lambda name: ctx.enter_context(nc.semaphore(name))
        sb = lambda c, name, shape, dt=F32: c.enter_context(nc.sbuf_tensor(name, shape, dt))
        ps = lambda c, name, shape, dt=F32: c.enter_context(nc.psum_tensor(name, shape, dt))

        q_parts_d = nc.dram_tensor("q_parts_d", (B, NPART, H * DQ, S), BF16).ap()
        k_parts_d = nc.dram_tensor("k_parts_d", (B, NPART, H * DQ, S), BF16).ap()
        o_d = nc.dram_tensor("o_d", (NG * GH * VW, S), F32).ap()

        x1 = sb(ctx, "x1", [P, NCH * TT, D])
        v_all = sb(ctx, "v_all", [P, B, HG, CPB, TT, GH * DV])
        w1 = sb(ctx, "w1", [P, 2, KT, HID], F32R)
        w2 = sb(ctx, "w2", [P, 2, MT, D], F32R)
        wo = sb(ctx, "wo", [P, 2, KT, D], F32R)
        b1_sb = sb(ctx, "b1_sb", [P, MT])
        hb2 = sb(ctx, "hb2", [P, D])
        ident = sb(ctx, "ident", [P, P])
        neg_half = sb(ctx, "neg_half", [P, TT])

        b_small = phase_b_small(nc, ctx, sb)

        with ExitStack() as actx:
            a = phase_a(nc, ctx, actx, sb, ps, x, x1, v_all, (w1t, w2t, wqkt, wvt, wot), (w1, w2, wo), (b1, b2, cos, sin),
                        b1_sb, hb2, ident, neg_half, q_parts_d, k_parts_d)
        with ExitStack() as bctx:
            b = phase_b(nc, ctx, bctx, sb, ps, b_small, v_all, q_parts_d, k_parts_d, o_d)
        with ExitStack() as cctx:
            c = phase_c(nc, ctx, cctx, sb, ps, b, x1, w1, w2, wo, b1_sb, hb2, ident, neg_half, o_d, out)
            block = cctx.enter_context(nc.Block())

            @block.sync
            def _(sp):
                load_first, attention = b.sync(sp)
                early, rest = c.sync(sp)
                a.sync(sp, load_first)
                a.signals["all_done"](sp)
                attention(early)
                rest()

            @block.gpsimd
            def _(pool):
                constants, first_buffers, first_split, attention = b.gpsimd(pool)
                a.gpsimd(pool, constants, first_buffers)
                first_split()
                a.signals["all_done"](pool)
                attention()
                c.gpsimd(pool)

            @block.scalar
            def _(act):
                early, rest = c.scalar(act)
                a.scalar(act)
                b.scalar(act, early)
                rest()

            @block.vector
            def _(dve):
                first_maxima, attention = b.vector(dve)
                a.vector(dve, first_maxima)
                attention()
                c.vector(dve)

            @block.tensor
            def _(pe):
                first_scores, attention = b.tensor(pe)
                early, rest = c.tensor(pe)
                a.tensor(pe, first_scores)
                attention(lambda: a.signals["all_done"](pe), early)
                rest()


def mm3(nc, out, w, acts, k, nk):
    for n, (pw, pa) in enumerate(PASSES):
        last = nc.tensor.matmul(out, w(pw), acts(pa), start=(k == 0 and n == 0),
                                stop=(k == nk - 1 and n == len(PASSES) - 1))
    return last


def phase_a(nc, sems, ctx, sb, ps, x, x1, v_all, weights_d, weights_kept, small_d, b1_sb, hb2, ident, neg_half,
            q_parts_d, k_parts_d):
    sem = lambda name: sems.enter_context(nc.semaphore(name))
    x_in = sb(ctx, "x_in", [P, TT, D])
    xt = [sb(ctx, "xt0", [P, 2, KT, CH], F32R)]
    NGB = 4
    g = sb(ctx, "g", [P, NGB, CH])
    shapes = [(KT, HID), (MT, D), (KT, 4 * P), (KT, D), (KT, D)]
    with ExitStack() as c:
        stage = [sb(c, f"stage{n}", [P, kt, w]) for n, (kt, w) in enumerate(shapes)]
    h = sb(ctx, "h", [P, 2, MT, CH], F32R)
    wqk = sb(ctx, "wqk", [P, 2, KT, 4 * P], F32R)
    wv = sb(ctx, "wv", [P, 2, KT, D], F32R)
    parts = sb(ctx, "parts", [P, 4, NPART, CH], BF16)
    res = sb(ctx, "res", [P, 2, CH])
    rot = sb(ctx, "rot", [P, CH])
    cos_sb = sb(ctx, "cos_sb", [P, S])
    sin_sb = sb(ctx, "sin_sb", [P, S])
    xn = sb(ctx, "xn", [P, TT, D])
    xt.append(sb(ctx, "xt1", [P, 2, KT, CH], F32R))
    stats = sb(ctx, "stats", [P, 2, TT, 6])
    mv = sb(ctx, "mv", [P, 2, TT, 2])
    rstd = sb(ctx, "rstd", [P, 2, TT])

    w1, w2, wo = weights_kept
    weights = [(src, dst, kt, w) for src, dst, (kt, w) in zip(weights_d, (w1, w2, wqk, wv, wo), shapes)]
    b1, b2, cos, sin = small_d
    small = [(b1_sb[:], b1), (hb2[:], b2.partition_broadcast(P)), (cos_sb[:], cos), (sin_sb[:], sin)]

    qkv_ps = ps(ctx, "qkv_ps", [P, 2, CH])
    tr_ps = ps(ctx, "tr_ps", [P, KT, CH])
    hid_ps = ps(ctx, "hid_ps", [P, 2, CH])
    y_ps = ps(ctx, "y_ps", [P, 2, CH])

    x_loaded = sem("x_loaded")
    stats_done = [sem(f"stats_done{n}") for n in range(2)]
    mean_ready = [sem(f"mean_ready{n}") for n in range(2)]
    ve_ready = [sem(f"ve_ready{n}") for n in range(2)]
    rstd_ready = [sem(f"rstd_ready{n}") for n in range(2)]
    xn_ready = [sem(f"xn_ready{n}") for n in range(2)]
    xt_ps_ready = [sem(f"xt_ps_ready{n}") for n in range(2)]
    xt_hi = [sem(f"xt_hi{n}") for n in range(2)]
    xt_lo = [sem(f"xt_lo{n}") for n in range(2)]
    base_ready, hid_done, gelu_done, h_hi, h_lo = (sem(n) for n in ("base_ready", "hid_done", "gelu_done", "h_hi", "h_lo"))
    y_done, x1_ready = sem("y_done"), sem("x1_ready")
    qkv_done, v_evac, rope_step = sem("qkv_done"), sem("v_evac"), sem("rope_step")
    part0, res_ready, part1, part2 = (sem(n) for n in ("part0", "res_ready", "part1", "part2"))
    stored = [sem(f"stored{n}") for n in range(4)]
    dve_passed, pool_passed = sem("a_dve_passed"), sem("a_pool_passed")

    w_loaded = [sem(f"w_loaded{n}") for n in range(len(weights))]
    w_hi, w_lo, small_loaded, consts, hb2_ready = (
        sem(n) for n in ("w_hi", "w_lo", "small_loaded", "consts", "hb2_ready"))

    def first_free(eng):
        eng.wait_ge(xn_ready[0], TT * NCH)
        eng.wait_ge(base_ready, TT * NCH)
        eng.wait_ge(hid_done, MT * NCH)
        eng.wait_ge(h_lo, MT * NCH)

    def all_done(eng):
        eng.wait_ge(y_done, TT * NCH)
        eng.wait_ge(x1_ready, TT * NCH)
        eng.wait_ge(qkv_done, 6 * NCH)
        eng.wait_ge(v_evac, 2 * NCH + 2)
        eng.wait_ge(part2, 4 * NCH)
        for i in range(4):
            eng.wait_ge(stored[i], 32 * (NCH + 1))

    x_v = x.rearrange("(n a p) d -> n p a d", a=TT, p=P)

    def sync(sp, load_first):
        def load(t):
            wait(sp, xn_ready[0], TT * t)
            wait(sp, base_ready, TT * t)
            sp.dma_start(x_in[:], x_v[bass.ds(t, 1)].rearrange("o p a d -> (o p) a d")).then_inc(x_loaded, 16)

        def store(s):
            for i in range(4):
                dst = (q_parts_d, k_parts_d)[i // 2].rearrange("b n (c j) q -> b j c n q", j=4)
                sp.wait_ge(part2, 4 * s + i + 1)
                for jj in range(2):
                    d = dst[bass.ds(s // CPB, 1), 2 * (i % 2) + jj, :, :, bass.ds((s % CPB) * CH, CH)]
                    sp.dma_start(d.rearrange("o c n q -> (o c) n q"),
                                 parts[64 * jj:64 * jj + 64, i]).then_inc(stored[i], 16)
        for i in range(4):
            sp.sem_inc(stored[i], 32)
        load(0)
        for n, (src, _, _, _) in enumerate(weights):
            sp.dma_start(stage[n][:], src.rearrange("(k p) n -> p k n", p=P)).then_inc(w_loaded[n], 16)
            if n == 1:
                for dst, src in small:
                    sp.dma_start(dst, src).then_inc(small_loaded, 16)
        load(1)
        with sp.Fori(1, NCH - 1) as t:
            load(t + 1)
            store(t - 1)
        first_free(sp)
        for i in range(4):
            sp.wait_ge(stored[i], 32 * (CPB + 1))
        load_first()
        store(NCH - 2)
        store(NCH - 1)

    def gpsimd(pool, constants, first_buffers):
        def rstd_of(n, t):
            hold(pool, mean_ready[n], TT * (t + 1), pool_passed)
            nc.gpsimd.tensor_scalar(rstd[:, n], mv[:, n, :, 1], EPS, None, ALU.add).then_inc(ve_ready[n], 1)
            pool.wait_ge(ve_ready[n], t + 1)
            nc.gpsimd.tensor_tensor(rstd[:, n], rstd[:, n], neg_half[:], ALU.pow).then_inc(rstd_ready[n], 1)

        def residual_base(t):
            hold(pool, x_loaded, 16 * (t + 1), pool_passed)
            for a in range(TT):
                nc.gpsimd.tensor_tensor(x1[:, bass.ds(TT * t + a, 1), :].rearrange("p o d -> p (o d)"),
                                        x_in[:, a], hb2[:], ALU.add).then_inc(base_ready, 1)

        nc.gpsimd.memset(ident[:], 0.0).then_inc(consts, 1)
        nc.gpsimd.memset(neg_half[:], -0.5).then_inc(consts, 1)
        pool.wait_ge(consts, 2)
        nc.gpsimd.affine_select(out=ident[:], in_=ident[:], compare_op=ALU.not_equal, fill=1.0,
                                base=0, pattern=[[-1, P]], channel_multiplier=1).then_inc(consts, 1)
        rstd_of(0, 0)
        pool.wait_ge(hb2_ready, 1)
        residual_base(0)
        constants()
        rstd_of(0, 1)
        residual_base(1)
        rstd_of(1, 0)
        with pool.Fori(1, NCH - 1) as t:
            rstd_of(0, t + 1)
            residual_base(t + 1)
            rstd_of(1, t)
        first_free(pool)
        pool.wait_ge(v_evac, 2 * CPB + 2)
        pool.sem_inc(pool_passed, 1)
        first_buffers()
        rstd_of(1, NCH - 1)

    def scalar(act):
        def hidden(t, m):
            act.wait_ge(hid_done, MT * t + m + 1)
            wait(act, h_lo, MT * t + m + 1 - NGB)
            nc.scalar.activation(g[:, m % NGB], hid_ps[:, m % 2], ACT.Gelu, bias=b1_sb[:, m:m + 1]).then_inc(gelu_done, 1)

        def upper(t, m):
            act.wait_ge(gelu_done, MT * t + m + 1)
            nc.scalar.activation(h[:, 0, m], g[:, m % NGB], ACT.Copy).then_inc(h_hi, 1)

        def gelus(t, ms):
            for m in ms:
                hidden(t, m)
                if m > ms[0]:
                    upper(t, m - 1)
            upper(t, ms[-1])

        def xt_upper(n, t):
            for k in range(KT):
                act.wait_ge(xt_ps_ready[n], KT * t + k + 1)
                nc.scalar.activation(xt[n][:, 0, k], tr_ps[:, k], ACT.Copy).then_inc(xt_hi[n], 1)

        def qkv_parts(s):
            for i in range(4):
                act.wait_ge(stored[i], 32 * (s + 1))
                if i % 2 == 0:
                    act.wait_ge(qkv_done, 6 * s + i + 1)
                    src = qkv_ps[:, i % 2]
                else:
                    act.wait_ge(rope_step, 8 * s + 4 * (i // 2) + 4)
                    src = rot[:]
                nc.scalar.activation(parts[:, i, 0], src, ACT.Copy).then_inc(part0, 1)
                act.wait_ge(res_ready, 4 * s + i + 1)
                nc.scalar.activation(parts[:, i, 1], res[:, i % 2], ACT.Copy).then_inc(part1, 1)
            for n in range(2):
                act.wait_ge(qkv_done, 6 * s + 5 + n)
                dst = v_all[:, bass.ds(s // CPB, 1), :, bass.ds(s % CPB, 1), 2 * n:2 * n + 2, :]
                nc.scalar.activation(dst.rearrange("p o g e a c -> p (o g) (e a) c"),
                                     qkv_ps[:, n].rearrange("p (a g c) -> p g a c", a=2, g=HG),
                                     ACT.Copy).then_inc(v_evac, 1)

        def body(t, first=False, last=False):
            gelus(t, range(0, MT // 2))
            if not first:
                xt_upper(1, t - 1)
            gelus(t, range(MT // 2, MT))
            if not last:
                xt_upper(0, t + 1)
            if not first:
                qkv_parts(t - 1)

        def weight_upper(n):
            act.wait_ge(w_loaded[n], 16)
            nc.scalar.activation(weights[n][1][:, 0], stage[n][:], ACT.Copy).then_inc(w_hi, 1)

        act.sem_inc(v_evac, 2)
        weight_upper(0)
        xt_upper(0, 0)
        act.wait_ge(small_loaded, 16 * len(small))
        nc.scalar.activation(hb2[:], hb2[:], ACT.Copy, scale=0.5).then_inc(hb2_ready, 1)
        for n in range(1, len(weights)):
            weight_upper(n)
        act.wait_ge(w_lo, 2)
        body(0, first=True)
        with act.Fori(1, NCH - 1) as t:
            body(t)
        body(NCH - 1, last=True)
        xt_upper(1, NCH - 1)
        qkv_parts(NCH - 1)

    def vector(dve, first_maxima):
        def src_of(n, t, a):
            return x_in[:, a] if n == 0 else x1[:, bass.ds(TT * t + a, 1), :].rearrange("p o d -> p (o d)")

        def ln_stats(n, t):
            hold(dve, xn_ready[n], TT * t, dve_passed)
            if n:
                hold(dve, x1_ready, TT * (t + 1), dve_passed)
            else:
                hold(dve, x_loaded, 16 * (t + 1), dve_passed)
            for a in range(TT):
                nc.vector.bn_stats(stats[:, n, a], src_of(n, t, a)).then_inc(stats_done[n], 1)
            for a in range(TT):
                hold(dve, stats_done[n], TT * t + a + 1, dve_passed)
                nc.vector.bn_aggr(mv[:, n, a], stats[:, n, a]).then_inc(mean_ready[n], 1)

        def ln_apply(n, t):
            if n == 0:
                wait(dve, xt_ps_ready[1], KT * (t - 1))
            else:
                dve.wait_ge(xt_ps_ready[0], KT * (t + 2) if not isinstance(t, int) else KT * min(t + 2, NCH))
            dve.wait_ge(rstd_ready[n], t + 1)
            for a in range(TT):
                nc.vector.tensor_scalar(xn[:, a], src_of(n, t, a), mv[:, n, a, 0:1], rstd[:, n, a:a + 1],
                                        ALU.subtract, ALU.mult).then_inc(xn_ready[n], 1)

        def h_lower(t, ms):
            for m in ms:
                dve.wait_ge(h_hi, MT * t + m + 1)
                nc.vector.tensor_tensor(h[:, 1, m], g[:, m % NGB], h[:, 0, m].bitcast(F32),
                                        ALU.subtract).then_inc(h_lo, 1)

        def xt_lower(n, t):
            for k in range(KT):
                dve.wait_ge(xt_hi[n], KT * t + k + 1)
                nc.vector.tensor_tensor(xt[n][:, 1, k], tr_ps[:, k], xt[n][:, 0, k].bitcast(F32),
                                        ALU.subtract).then_inc(xt_lo[n], 1)

        def part_two(s, i):
            dve.wait_ge(part1, 4 * s + i + 1)
            nc.vector.tensor_tensor(parts[:, i, 2], res[:, i % 2], parts[:, i, 1],
                                    ALU.subtract).then_inc(part2, 1)

        def qkv_parts(s, beside=None):
            for i in range(4):
                if beside:
                    beside(i)
                if i % 2:
                    dve.wait_ge(qkv_done, 6 * s + i + 1)
                    at = bass.ds((s % CPB) * CH, CH)
                    step = 8 * s + 4 * (i // 2)
                    if i == 3:
                        dve.wait_ge(part2, 4 * s + 2)
                    nc.vector.tensor_tensor(rot[:], qkv_ps[:, 1], cos_sb[:, at], ALU.mult).then_inc(rope_step, 1)
                    nc.vector.tensor_tensor(res[0:64, 1], qkv_ps[64:128, 1], sin_sb[64:128, at], ALU.mult).then_inc(rope_step, 1)
                    nc.vector.tensor_tensor(res[64:128, 1], qkv_ps[0:64, 1], sin_sb[0:64, at], ALU.mult).then_inc(rope_step, 1)
                    dve.wait_ge(rope_step, step + 3)
                    nc.vector.tensor_tensor(rot[:], rot[:], res[:, 1], ALU.add).then_inc(rope_step, 1)
                dve.wait_ge(part0, 4 * s + i + 1)
                src = rot[:] if i % 2 else qkv_ps[:, 0]
                if i >= 2:
                    dve.wait_ge(part2, 4 * s + i - 1)
                nc.vector.tensor_tensor(res[:, i % 2], src, parts[:, i, 0], ALU.subtract).then_inc(res_ready, 1)
                if i:
                    part_two(s, i - 1)
            part_two(s, 3)
            dve.wait_ge(part2, 4 * s + 4)

        def residual(t):
            dve.wait_ge(base_ready, TT * (t + 1))
            for a in range(TT):
                dve.wait_ge(y_done, TT * t + 2 * (a // 2) + 2)
                place = x1[:, bass.ds(TT * t + a, 1), :].rearrange("p o d -> p (o d)")
                nc.vector.scalar_tensor_tensor(place, y_ps[:, a // 2, (a % 2) * D:(a % 2 + 1) * D], 0.5, place,
                                               ALU.mult, ALU.add).then_inc(x1_ready, 1)

        def body(t, first=False, last=False):
            h_lower(t, range(0, MT // 2))
            if not last:
                ln_stats(0, t + 1)
            if not first:
                xt_lower(1, t - 1)
            if not last:
                ln_apply(0, t + 1)
            h_lower(t, range(MT // 2, MT))
            if not last:
                xt_lower(0, t + 1)
            if not first:
                qkv_parts(t - 1)
            residual(t)
            ln_stats(1, t)
            if last:
                first_maxima(0)
                first_maxima(1)
            ln_apply(1, t)

        def weight_lower(n):
            dve.wait_ge(w_hi, n + 1)
            nc.vector.tensor_tensor(weights[n][1][:, 1], stage[n][:], weights[n][1][:, 0].bitcast(F32),
                                    ALU.subtract).then_inc(w_lo, 1)

        ln_stats(0, 0)
        ln_apply(0, 0)
        weight_lower(0)
        xt_lower(0, 0)
        for n in range(1, len(weights)):
            weight_lower(n)
        dve.wait_ge(w_lo, len(weights))
        dve.wait_ge(small_loaded, 16 * len(small))
        body(0, first=True)
        with dve.Fori(1, NCH - 1) as t:
            body(t)
        body(NCH - 1, last=True)
        first_maxima(2)
        xt_lower(1, NCH - 1)

        def beside(i):
            for k in ((3, 4, 5), (6, 7), (8, 9), (10, 11))[i]:
                first_maxima(k)

        qkv_parts(NCH - 1, beside)

    def tensor(pe, first_scores):
        def transposes(n, t):
            pe.wait_ge(xn_ready[n], TT * (t + 1))
            if n == 0:
                wait(pe, xt_lo[1], KT * (t - 1))
            else:
                wait(pe, xt_lo[0], KT * (t + 2) if not isinstance(t, int) else KT * min(t + 2, NCH))
            for k in range(KT):
                for a in range(TT):
                    last = nc.tensor.transpose(tr_ps[:, k, P * a:P * (a + 1)], xn[:, a, P * k:P * (k + 1)], ident[:])
                last.then_inc(xt_ps_ready[n], 1)

        def ffn_up(t, ms):
            pe.wait_ge(xt_lo[0], KT * (t + 1))
            for m in ms:
                wait(pe, gelu_done, MT * t + m - 1)
                for k in range(KT):
                    last = mm3(nc, hid_ps[:, m % 2], lambda p: w1[:, p, k, P * m:P * (m + 1)],
                               lambda p: xt[0][:, p, k], k, KT)
                last.then_inc(hid_done, 1)

        def ffn_down(t, a):
            if a == 0:
                if isinstance(t, int) and t == 0:
                    pe.wait_ge(w_lo, len(weights))
                wait(pe, x1_ready, TT * t)
            for k in range(MT):
                if a == 0:
                    pe.wait_ge(h_lo, MT * t + k + 1)
                last = mm3(nc, y_ps[:, a // 2, (a % 2) * D:(a % 2 + 1) * D],
                           lambda p: h[:, p, k, P * a:P * (a + 1)], lambda p: w2[:, p, k], k, MT)
            last.then_inc(y_done, 1)

        def qk(s, m):
            if m == 0:
                pe.wait_ge(xt_lo[1], KT * (s + 1))
            if m < 2:
                pe.wait_ge(v_evac, 2 * s + m + 1)
            else:
                pe.wait_ge(res_ready, 4 * s + m - 1)
            for k in range(KT):
                last = mm3(nc, qkv_ps[:, m % 2], lambda p: wqk[:, p, k, P * m:P * (m + 1)],
                           lambda p: xt[1][:, p, k], k, KT)
            last.then_inc(qkv_done, 1)

        def values(s, n):
            pe.wait_ge(res_ready, 4 * s + 3 + n)
            for a in range(2):
                for k in range(KT):
                    tile = 2 * n + a
                    last = mm3(nc, qkv_ps[:, n, a * D:(a + 1) * D],
                               lambda p: xt[1][:, p, k, P * tile:P * (tile + 1)],
                               lambda p: wv[:, p, k], k, KT)
            last.then_inc(qkv_done, 1)

        def body(t, first=False, last=False):
            ffn_up(t, range(0, MT // 2))
            if not first:
                transposes(1, t - 1)
            ffn_up(t, range(MT // 2, MT))
            if not last:
                transposes(0, t + 1)
            for a in range(TT):
                if not first:
                    if a == 0:
                        qk(t - 1, 0)
                        qk(t - 1, 1)
                    elif a < 3:
                        qk(t - 1, a + 1)
                    else:
                        values(t - 1, 0)
                ffn_down(t, a)
            if not first:
                values(t - 1, 1)

        pe.wait_ge(consts, 3)
        transposes(0, 0)
        pe.wait_ge(w_lo, 1)
        body(0, first=True)
        with pe.Fori(1, NCH - 1) as t:
            body(t)
        body(NCH - 1, last=True)
        pe.wait_ge(gelu_done, MT * NCH)
        pe.wait_ge(x1_ready, TT * NCH)
        for k in range(3):
            first_scores(k)
        transposes(1, NCH - 1)
        first_scores(3)
        first_scores(4)
        first_scores(5)
        qk(NCH - 1, 0)
        first_scores(6)
        qk(NCH - 1, 1)
        first_scores(7)
        qk(NCH - 1, 2)
        first_scores(8)
        first_scores(9)
        qk(NCH - 1, 3)
        first_scores(10)
        first_scores(11)
        values(NCH - 1, 0)
        first_scores(12)
        values(NCH - 1, 1)

    return Programs(sync, gpsimd, scalar, vector, tensor, all_done=all_done)


FIRST = 12


def phase_b_small(nc, ctx, sb):
    ident_bf = sb(ctx, "ident_bf", [P, P], BF16)
    mask_bf = sb(ctx, "mask_bf", [P, P], BF16)
    mask_t_bf = sb(ctx, "mask_t_bf", [P, P], BF16)
    nmax = [sb(ctx, f"nmax{n}", [P, GH, 4]) for n in range(2)]
    pmax = sb(ctx, "pmax", [P, GH, 4, 2])
    n_res = [sb(ctx, f"n_res{n}", [P, GH, 4]) for n in range(2)]
    n_part = [sb(ctx, f"n_part{n}", [P, NPART, GH, 4], BF16) for n in range(2)]
    n_row = [sb(ctx, f"n_row{n}", [NPART * GH * 4, P], BF16) for n in range(2)]
    return ident_bf, mask_bf, mask_t_bf, nmax, pmax, n_res, n_part, n_row


def phase_b(nc, sems, ctx, sb, ps, small, v_all, q_parts_d, k_parts_d, o_d):
    sem = lambda name: sems.enter_context(nc.semaphore(name))
    q_st, k_st, va, probs = [], [], [], []
    for n in range(RING):
        q_st.append(sb(ctx, f"q_st{n}", [P, 2, GH, CH], BF16))
        k_st.append(sb(ctx, f"k_st{n}", [P, GH, S], BF16))
        va.append(sb(ctx, f"va{n}", [P, QT, GH, VW]))
        if n == 0:
            probs = [sb(ctx, f"probs{m}", [P, GH, CH]) for m in range(RING)]
    ident_bf, mask_bf, mask_t_bf, nmax, pmax, n_res, n_part, n_row = small
    o_sb = [sb(ctx, f"o_sb{n}", [P, CH]) for n in range(2)]

    st_ps = [ps(ctx, f"st_ps{n}", [P, 2, CH]) for n in range(2)]
    s_ps = ps(ctx, "s_ps", [P, BANKS, CH])
    pv_ps = ps(ctx, "pv_ps", [P, CH])

    loaded = [sem(f"stack_loaded{n}") for n in range(RING)]
    consts, ones_rows, va_ready = sem("b_consts"), sem("ones_rows"), sem("va_ready")
    s_done, max_done, nmax1_ready = sem("s_done"), sem("max_done"), sem("nmax1_ready")
    nt_done, n_row_ready, split_step = sem("nt_done"), sem("n_row_ready"), sem("split_step")
    m_rows = [sem(f"m_rows{n}") for n in range(2)]
    st_done, exp_done, pv_done = (sem(n) for n in ("st_done", "exp_done", "pv_done"))
    o_ready, pool_passed = sem("o_ready"), sem("b_pool_passed")
    o_stored = [sem(f"o_stored{n}") for n in range(2)]
    NCONST = 6
    PER_LOAD = 16 * 3 * NB

    qs_v = q_parts_d.rearrange("b n (e h r) q -> b n e r h q", h=GH, r=DQ)
    ks_v = k_parts_d.rearrange("b n (e h r) q -> b n e r h q", h=GH, r=DQ)
    o_v = o_d.rearrange("(g p) q -> g p q", p=P)
    v_v = v_all[:].rearrange("p b g c a w -> p (b g) (c a) w")

    def groups(eng, body):
        body(0, 0)
        with eng.Fori(0, (NG - 1) // RING - 1) as i:
            for r in range(1, RING + 1):
                body(RING * i + r, r % RING)
        for g in range(NG - RING, NG):
            body(g, g % RING)

    def is_last(g):
        return isinstance(g, int) and g == NG - 1

    def sync(sp):
        def load(g, r):
            for n in range(NB):
                rows = slice(DQ * n, DQ * (n + 1))
                src = ks_v[bass.ds(g // HG, 1), K_BLOCKS[n], bass.ds(g % HG, 1)]
                sp.dma_start(k_st[r][rows], src.rearrange("o e r h q -> (o e r) h q")).then_inc(loaded[r], 16)
                for half in range(2):
                    src = qs_v[bass.ds(g // HG, 1), Q_BLOCKS[n], bass.ds(g % HG, 1), :, :, CH * half:CH * (half + 1)]
                    sp.dma_start(q_st[r][rows, half], src.rearrange("o e r h q -> (o e r) h q")).then_inc(loaded[r], 16)

        def max_rows(half, g, r):
            sp.wait_ge(n_row_ready, 2 * g + half + 1)
            sp.dma_start(q_st[r][ROWS:ROWS_M, half].rearrange("p h (t q) -> p (h t) q", q=P),
                         n_row[half][:]).then_inc(m_rows[half], 16)

        def store(c, g):
            sp.wait_ge(o_ready, 2 * g + c + 1)
            sp.dma_start(o_v[bass.ds(g, 1), :, CH * c:CH * (c + 1)].rearrange("o p q -> (o p) q"),
                         o_sb[c][:]).then_inc(o_stored[c], 16)

        def body(g, r, steps):
            max_rows(1, g, r)
            if not isinstance(g, int) or g + 2 < NG:
                sp.wait_ge(st_done, 2 * NU * g + 1)
                load(g + 2, (r + 2) % RING)
            if isinstance(g, int) and g in steps:
                sp.wait_ge(st_done, 2 * NU * g + 1)
                steps[g]()
            if not isinstance(g, int) or g + 1 < NG:
                max_rows(0, g + 1, (r + 1) % RING)
            store(0, g)
            store(1, g)

        def main(steps):
            load(1, 1)
            max_rows(0, 0, 0)
            groups(sp, lambda g, r: body(g, r, steps))
            for c in range(2):
                sp.wait_ge(o_stored[c], 16 * NG)

        return lambda: load(0, 0), main

    def gpsimd(pool):
        def constants():
            nc.gpsimd.memset(ident_bf[:], 0.0).then_inc(consts, 1)
            nc.gpsimd.memset(mask_bf[:], 0.0).then_inc(consts, 1)
            nc.gpsimd.memset(mask_t_bf[:], 0.0).then_inc(consts, 1)
            pool.wait_ge(consts, 3)
            nc.gpsimd.affine_select(out=mask_t_bf[:], in_=mask_t_bf[:], compare_op=ALU.is_ge, fill=NEG, base=0,
                                    pattern=[[1, P]], channel_multiplier=-1).then_inc(consts, 1)
            nc.gpsimd.affine_select(out=ident_bf[:], in_=ident_bf[:], compare_op=ALU.not_equal, fill=1.0, base=0,
                                    pattern=[[-1, P]], channel_multiplier=1).then_inc(consts, 1)
            nc.gpsimd.affine_select(out=mask_bf[:], in_=mask_bf[:], compare_op=ALU.is_ge, fill=NEG, base=0,
                                    pattern=[[-1, P]], channel_multiplier=1).then_inc(consts, 1)

        def ones(r):
            nc.gpsimd.memset(k_st[r][ROWS:ROWS_M], 1.0).then_inc(ones_rows, 1)
            pool.wait_ge(ones_rows, 2 * r + 1)
            nc.gpsimd.memset(va[r][:, :, :, DV:VW], 1.0).then_inc(ones_rows, 1)
            hold(pool, ones_rows, 2 * r + 2, pool_passed)

        def values(g, r):
            nc.gpsimd.tensor_copy(va[r][:, :, :, 0:DV],
                                  v_v[:, bass.ds(g, 1), :, :].rearrange("p o j (h d) -> p (o j) h d", h=GH)
                                  ).then_inc(va_ready, 1)

        def split(half, g):
            k = 2 * g + half
            wait(pool, nt_done, k - 1)
            if half == 0:
                hold(pool, max_done, NI * g + FIRST_HALF, pool_passed)
            else:
                hold(pool, nmax1_ready, g + 1, pool_passed)
            nc.gpsimd.tensor_copy(n_part[half][:, 0], nmax[half][:]).then_inc(split_step, 1)
            pool.wait_ge(split_step, 4 * k + 1)
            nc.gpsimd.tensor_tensor(n_res[half][:], nmax[half][:], n_part[half][:, 0], ALU.subtract).then_inc(split_step, 1)
            hold(pool, split_step, 4 * k + 2, pool_passed)
            nc.gpsimd.tensor_copy(n_part[half][:, 1], n_res[half][:]).then_inc(split_step, 1)
            pool.wait_ge(split_step, 4 * k + 3)
            nc.gpsimd.tensor_tensor(n_part[half][:, 2], n_res[half][:], n_part[half][:, 1], ALU.subtract).then_inc(split_step, 1)

        def body(g, r):
            split(1, g)
            if not is_last(g):
                values(g + 1, (r + 1) % RING)
                split(0, g + 1)

        def first_buffers():
            ones(0)
            values(0, 0)

        def main():
            pool.wait_ge(split_step, 4)
            ones(1)
            ones(2)
            groups(pool, body)

        return constants, first_buffers, lambda: split(0, 0), main

    def vector(dve):
        def maxima(g, k, r):
            i, part, heads, _, w = ITEMS[k]
            dve.wait_ge(s_done, NI * g + k + 1)
            bank = (r + STREAM.index(("S", k))) % BANKS
            src = s_ps[:, bank, 0:w * len(heads)].rearrange("p (h k) -> p h k", k=w)
            h0, h1 = heads[0], heads[-1] + 1
            if i < 4:
                nc.vector.tensor_reduce(nmax[0][:, h0:h1, i], src, axis=AX.X, op=ALU.max, negate=True).then_inc(max_done, 1)
            else:
                nc.vector.tensor_reduce(pmax[:, h0:h1, i - 4, part], src, axis=AX.X, op=ALU.max).then_inc(max_done, 1)

        def all_maxima(g, r, first=0):
            for k in range(first, NI):
                maxima(g, k, r)
            dve.wait_ge(max_done, NI * (g + 1))
            nc.vector.tensor_reduce(nmax[1][:], pmax[:], axis=AX.X, op=ALU.max, negate=True).then_inc(nmax1_ready, 1)

        def body(g, r):
            if not is_last(g):
                all_maxima(g + 1, (r + 1) % RING)

        def main():
            all_maxima(0, 0, FIRST)
            groups(dve, body)

        return lambda k: maxima(0, k, 0), main

    def scalar(act, steps):
        def row(half, g, r):
            bank = (r + STREAM.index((f"T{half}", 0))) % BANKS
            act.wait_ge(nt_done, 2 * g + half + 1)
            wait(act, m_rows[half], 16 * g)
            nc.scalar.activation(n_row[half][:], s_ps[0:NPART * GH * 4, bank, 0:P], ACT.Copy).then_inc(n_row_ready, 1)

        def exps(g, u, r):
            _, w = unit_span(*UNITS[u])
            for hp in range(2):
                act.wait_ge(st_done, 2 * (NU * g + u) + hp + 1)
                if hp == 0:
                    wait(act, pv_done, NU * g + u - RING + 1)
                nc.scalar.activation(probs[u % RING][:, 2 * hp:2 * hp + 2, 0:w], st_ps[hp][:, :, 0:w], ACT.Exp,
                                     scale=SCALE).then_inc(exp_done, 1)
                if (u, hp) == T_AT[1]:
                    row(1, g, (r + 1) % RING)
                if (u, hp) == T_AT[0] and not is_last(g):
                    row(0, g + 1, (r + 1) % RING)

        def evacuate(c, g):
            last_unit = 3 if c == 0 else NU - 1
            act.wait_ge(pv_done, NU * g + last_unit + 1)
            wait(act, o_stored[c], 16 * g)
            nc.scalar.activation(o_sb[c][:], pv_ps[:], ACT.Copy).then_inc(o_ready, 1)

        def body(g, r):
            for u in range(NU):
                exps(g, u, r)
                if is_last(g) and u in steps:
                    steps[u]()
                if u == 4:
                    evacuate(0, g)
                if u == 0 and not (isinstance(g, int) and g == 0):
                    evacuate(1, g - 1)
            if is_last(g):
                evacuate(1, g)

        row(0, 0, 0)
        groups(act, body)

    def tensor(pe):
        def slot_free(g, x):
            if isinstance(g, int) and g == NG:
                return
            y = x - BANKS
            g, y = (g, y) if y >= 0 else (g - 1, y + NS)
            kind, k = STREAM[y]
            if isinstance(g, int) and (g < 0 or (g == 0 and kind == "T1")):
                return
            if kind == "S":
                pe.wait_ge(max_done, NI * g + k + 1)
            elif kind == "T0":
                pe.wait_ge(n_row_ready, 2 * g + 1)
            else:
                pe.wait_ge(n_row_ready, 2 * (g - 1) + 2)

        def stream(g, x, r):
            kind, k = STREAM[x]
            bank = (r + x) % BANKS
            slot_free(g, x)
            if kind == "S":
                _, _, heads, k0, w = ITEMS[k]
                i = ITEMS[k][0]
                for n, hd in enumerate(heads):
                    o = s_ps[:, bank, n * w:(n + 1) * w]
                    diagonal = k0 + w == P * (i + 1)
                    last = nc.tensor.matmul(o, q_st[r][0:ROWS, i // 4, hd, P * (i % 4):P * (i % 4 + 1)],
                                            k_st[r][0:ROWS, hd, k0:k0 + w], start=True, stop=not diagonal)
                    if diagonal:
                        last = nc.tensor.matmul(o[:, w - P:w], ident_bf[:], mask_bf[:], start=False, stop=True)
                last.then_inc(s_done, 1)
                return
            half = int(kind[1])
            pe.wait_ge(split_step, 8 * g + 4 if kind == "T0" else 8 * g)
            nc.tensor.matmul(s_ps[0:NPART * GH * 4, bank, 0:P], n_part[half][:].rearrange("p n h t -> p (n h t)"),
                             ident_bf[:], start=True, stop=True).then_inc(nt_done, 1)

        def scores(g, u, hp, r):
            c, j = UNITS[u]
            q0, w = unit_span(c, j)
            if j == 0 and hp == 0:
                pe.wait_ge(m_rows[c], 16 * (g + 1))
            wait(pe, exp_done, 2 * (NU * g + u) + hp - 1)
            for n in range(2):
                hd = 2 * hp + n
                last = nc.tensor.matmul(st_ps[hp][:, n, 0:w], k_st[r][0:ROWS_M, hd, P * j:P * (j + 1)],
                                        q_st[r][0:ROWS_M, c, hd, q0 - CH * c:q0 - CH * c + w],
                                        start=True, stop=u not in DIAG)
                if u in DIAG:
                    last = nc.tensor.matmul(st_ps[hp][:, n, 0:P], ident_bf[:], mask_t_bf[:], start=False, stop=True)
            last.then_inc(st_done, 1)

        def sums(g, u, r):
            c, j = UNITS[u]
            q0, w = unit_span(c, j)
            pe.wait_ge(exp_done, 2 * (NU * g + u) + 2)
            if j == 0:
                wait(pe, o_ready, 2 * g + c)
                if c == 0:
                    pe.wait_ge(va_ready, g + 1)
            for hd in range(GH):
                last = nc.tensor.matmul(pv_ps[VW * hd:VW * (hd + 1), q0 - CH * c:q0 - CH * c + w],
                                        va[r][:, j, hd, :], probs[u % RING][:, hd, 0:w],
                                        start=j == 0, stop=j == 4 * (c + 1) - 1)
            last.then_inc(pv_done, 1)

        def body(g, r, steps):
            nxt = (r + 1) % RING

            def stream_step(u, n):
                for x in STEPS[3 * u + n]:
                    if x == 0 and not is_last(g):
                        pe.wait_ge(loaded[nxt], PER_LOAD * ((g + 1) // RING + 1))
                    if not is_last(g) or STREAM[x][0] == "T1":
                        stream(g + 1, x, nxt)

            for u in range(NU):
                scores(g, u, 0, r)
                stream_step(u, 0)
                scores(g, u, 1, r)
                stream_step(u, 1)
                if u:
                    sums(g, u - 1, r)
                elif not (isinstance(g, int) and g == 0):
                    sums(g - 1, NU - 1, (r - 1) % RING)
                stream_step(u, 2)
                if is_last(g) and u in steps:
                    steps[u]()
            if is_last(g):
                sums(g, NU - 1, r)

        def first_scores(k):
            if k == 0:
                pe.wait_ge(consts, NCONST)
                pe.wait_ge(loaded[0], PER_LOAD)
            stream(0, STREAM.index(("S", k)), 0)

        def main(banks_free, steps):
            for x in range(STREAM.index(("S", FIRST)) + 1, NS):
                stream(0, x, 0)
            banks_free()
            pe.wait_ge(ones_rows, 2 * RING)
            groups(pe, lambda g, r: body(g, r, steps))

        return first_scores, main

    return Programs(sync, gpsimd, scalar, vector, tensor, o_stored=o_stored, o_ready=o_ready, n_row_ready=n_row_ready)


T_AT = {n: next((k // 3, min(k % 3, 1)) for k in range(3 * NU) if STREAM.index((f"T{n}", 0)) in STEPS[k])
        for n in range(2)}


def phase_c(nc, sems, ctx, sb, ps, b, x1, w1, w2, wo, b1_sb, hb2, ident, neg_half, o_d, out):
    sem = lambda name: sems.enter_context(nc.semaphore(name))
    h = sb(ctx, "c_h", [P, 2, MT, CH], F32R)
    NGB = 4
    g = sb(ctx, "c_g", [P, NGB, CH])
    y = sb(ctx, "c_y", [P, TT, D])
    num = sb(ctx, "num", [P, KT, CH])
    den = sb(ctx, "den", [P, KT, CH])
    rden = sb(ctx, "rden", [P, KT, CH])
    att = sb(ctx, "att", [P, KT, CH])
    xn = sb(ctx, "c_xn", [P, TT, D])
    att_p = sb(ctx, "att_p", [P, 2, KT, CH], F32R)
    xt = sb(ctx, "c_xt", [P, 2, KT, CH], F32R)
    stats = sb(ctx, "c_stats", [P, TT, 6])
    mv = sb(ctx, "c_mv", [P, TT, 2])
    ve = sb(ctx, "c_ve", [P, TT])
    rstd = sb(ctx, "c_rstd", [P, TT])

    hid_ps = ps(ctx, "c_hid_ps", [P, 2, CH])
    y_ps = ps(ctx, "c_y_ps", [P, 2, CH])
    wo_ps = ps(ctx, "c_wo_ps", [P, 2, CH])
    tr_ps = ps(ctx, "c_tr_ps", [P, KT, CH])

    o_loaded, rden_ready, att_ready, att_hi, att_lo, wo_done, x2_ready = (
        sem(n) for n in ("o_loaded", "rden_ready", "att_ready", "att_hi", "att_lo", "wo_done", "x2_ready"))
    stats_done, mean_ready, ve_ready, rstd_ready, xn_ready = (
        sem(n) for n in ("c_stats_done", "c_mean_ready", "c_ve_ready", "c_rstd_ready", "c_xn_ready"))
    xt_ps_ready, xt_hi, xt_lo, base_ready = (sem(n) for n in ("c_xt_ps_ready", "c_xt_hi", "c_xt_lo", "c_base_ready"))
    hid_done, gelu_done, h_hi, h_lo = (sem(n) for n in ("c_hid_done", "c_gelu_done", "c_h_hi", "c_h_lo"))
    y_done, y_ready, y_stored = sem("c_y_done"), sem("c_y_ready"), sem("c_y_stored")
    dve_passed, pool_passed = sem("c_dve_passed"), sem("c_pool_passed")

    o_v = o_d.rearrange("(b k e s r) q -> b k s e r q", b=B, k=KT, s=2, r=DV)
    out_v = out.rearrange("(n a p) d -> n p a d", a=TT, p=P)

    def sync(sp):
        def load(t):
            wait(sp, att_ready, t)
            for k in range(KT):
                for s, dst in ((0, num), (1, den)):
                    src = o_v[bass.ds(t // CPB, 1), k, s, :, :, bass.ds((t % CPB) * CH, CH)]
                    sp.dma_start(dst[:, k, :], src.rearrange("o e r q -> (o e) r q")).then_inc(o_loaded, 16)

        def store(t):
            sp.wait_ge(y_ready, TT * (t + 1))
            sp.dma_start(out_v[bass.ds(t, 1)].rearrange("o p a d -> (o p) a d"), y[:]).then_inc(y_stored, 16)

        def early(t):
            sp.wait_ge(b.signals["o_stored"][t], 16 * HG)
            load(t)

        def main():
            load(2)
            store(0)
            with sp.Fori(1, NCH - 2) as t:
                load(t + 2)
                store(t)
            store(NCH - 2)
            store(NCH - 1)
            sp.wait_ge(y_stored, 16 * NCH)

        return {NG - 2: lambda: early(0), NG - 1: lambda: early(1)}, main

    def gpsimd(pool):
        def norm(t):
            hold(pool, mean_ready, TT * (t + 1), pool_passed)
            nc.gpsimd.tensor_scalar(ve[:], mv[:, :, 1], EPS, None, ALU.add).then_inc(ve_ready, 1)
            pool.wait_ge(ve_ready, t + 1)
            nc.gpsimd.tensor_tensor(rstd[:], ve[:], neg_half[:], ALU.pow).then_inc(rstd_ready, 1)

        def residual_base(t):
            hold(pool, xn_ready, TT * (t + 1), pool_passed)
            for a in range(TT):
                place = x1[:, bass.ds(TT * t + a, 1), :].rearrange("p o d -> p (o d)")
                nc.gpsimd.tensor_tensor(place, place, hb2[:], ALU.add).then_inc(base_ready, 1)

        norm(0)
        residual_base(0)
        norm(1)
        residual_base(1)
        with pool.Fori(1, NCH - 1) as t:
            norm(t + 1)
            residual_base(t + 1)

    def scalar(act):
        def hidden(t, m):
            act.wait_ge(hid_done, MT * t + m + 1)
            wait(act, h_lo, MT * t + m + 1 - NGB)
            nc.scalar.activation(g[:, m % NGB], hid_ps[:, m % 2], ACT.Gelu, bias=b1_sb[:, m:m + 1]).then_inc(gelu_done, 1)

        def upper(t, m):
            act.wait_ge(gelu_done, MT * t + m + 1)
            nc.scalar.activation(h[:, 0, m], g[:, m % NGB], ACT.Copy).then_inc(h_hi, 1)

        def gelus(t, ms):
            for m in ms:
                hidden(t, m)
                if m > ms[0]:
                    upper(t, m - 1)
            upper(t, ms[-1])

        def xt_upper(t):
            for k in range(KT):
                act.wait_ge(xt_ps_ready, KT * t + k + 1)
                nc.scalar.activation(xt[:, 0, k], tr_ps[:, k], ACT.Copy).then_inc(xt_hi, 1)

        def att_upper(t):
            act.wait_ge(att_ready, t + 1)
            wait(act, wo_done, TT * t)
            nc.scalar.activation(att_p[:, 0], att[:], ACT.Copy).then_inc(att_hi, 1)

        def body(t, nxt=True, second=True):
            gelus(t, range(MT // 2))
            gelus(t, range(MT // 2, MT))
            if nxt:
                xt_upper(t + 1)
            if second:
                att_upper(t + 2)

        def main():
            att_upper(1)
            xt_upper(0)
            body(0)
            with act.Fori(1, NCH - 2) as t:
                body(t)
            body(NCH - 2, second=False)
            body(NCH - 1, nxt=False, second=False)

        return {4: lambda: att_upper(0)}, main

    def vector(dve):
        def x1_tile(t, a):
            return x1[:, bass.ds(TT * t + a, 1), :].rearrange("p o d -> p (o d)")

        def attention_rows(t):
            dve.wait_ge(o_loaded, 64 * (t + 1))
            wait(dve, att_lo, t)
            for k in range(KT):
                nc.vector.reciprocal(rden[:, k], den[:, k]).then_inc(rden_ready, 1)
            dve.wait_ge(rden_ready, KT * (t + 1))
            nc.vector.tensor_tensor(att[:], num[:], rden[:], ALU.mult).then_inc(att_ready, 1)

        def att_lower(t):
            dve.wait_ge(att_hi, t + 1)
            nc.vector.tensor_tensor(att_p[:, 1], att[:], att_p[:, 0].bitcast(F32), ALU.subtract).then_inc(att_lo, 1)

        def residual_attention(t):
            for a in range(TT):
                dve.wait_ge(wo_done, TT * t + 2 * (a // 2) + 2)
                nc.vector.tensor_tensor(x1_tile(t, a), wo_ps[:, a // 2, (a % 2) * D:(a % 2 + 1) * D],
                                        x1_tile(t, a), ALU.add).then_inc(x2_ready, 1)

        def statistics(t):
            hold(dve, xn_ready, TT * t, dve_passed)
            for a in range(TT):
                hold(dve, x2_ready, TT * t + a + 1, dve_passed)
                nc.vector.bn_stats(stats[:, a], x1_tile(t, a)).then_inc(stats_done, 1)
            for a in range(TT):
                hold(dve, stats_done, TT * t + a + 1, dve_passed)
                nc.vector.bn_aggr(mv[:, a], stats[:, a]).then_inc(mean_ready, 1)

        def normalize(t):
            dve.wait_ge(rstd_ready, t + 1)
            wait(dve, xt_ps_ready, KT * t)
            for a in range(TT):
                nc.vector.tensor_scalar(xn[:, a], x1_tile(t, a), mv[:, a, 0:1], rstd[:, a:a + 1],
                                        ALU.subtract, ALU.mult).then_inc(xn_ready, 1)

        def h_lower(t, ms):
            for m in ms:
                dve.wait_ge(h_hi, MT * t + m + 1)
                nc.vector.tensor_tensor(h[:, 1, m], g[:, m % NGB], h[:, 0, m].bitcast(F32),
                                        ALU.subtract).then_inc(h_lo, 1)

        def xt_lower(t):
            for k in range(KT):
                dve.wait_ge(xt_hi, KT * t + k + 1)
                nc.vector.tensor_tensor(xt[:, 1, k], tr_ps[:, k], xt[:, 0, k].bitcast(F32),
                                        ALU.subtract).then_inc(xt_lo, 1)

        def residual(t):
            dve.wait_ge(base_ready, TT * (t + 1))
            wait(dve, y_stored, 16 * t)
            for a in range(TT):
                dve.wait_ge(y_done, TT * t + 2 * (a // 2) + 2)
                nc.vector.scalar_tensor_tensor(y[:, a], y_ps[:, a // 2, (a % 2) * D:(a % 2 + 1) * D], 0.5,
                                               x1_tile(t, a), ALU.mult, ALU.add).then_inc(y_ready, 1)

        def body(t, nxt=True, second=True):
            h_lower(t, range(1))
            if nxt:
                residual_attention(t + 1)
                statistics(t + 1)
            h_lower(t, range(1, MT // 2))
            if nxt:
                normalize(t + 1)
            h_lower(t, range(MT // 2, MT))
            if nxt:
                xt_lower(t + 1)
            if second:
                attention_rows(t + 2)
                att_lower(t + 2)
            residual(t)

        attention_rows(0)
        att_lower(0)
        attention_rows(1)
        residual_attention(0)
        statistics(0)
        normalize(0)
        att_lower(1)
        xt_lower(0)
        body(0)
        with dve.Fori(1, NCH - 2) as t:
            body(t)
        body(NCH - 2, second=False)
        body(NCH - 1, nxt=False, second=False)

    def tensor(pe):
        def project(t, tiles=range(TT)):
            if isinstance(t, int) and t == 0:
                pe.wait_ge(b.signals["n_row_ready"], 2 * NG)
            pe.wait_ge(att_lo, t + 1)
            wait(pe, x2_ready, TT * t)
            for a in tiles:
                for k in range(KT):
                    last = mm3(nc, wo_ps[:, a // 2, (a % 2) * D:(a % 2 + 1) * D],
                               lambda p: att_p[:, p, k, P * a:P * (a + 1)], lambda p: wo[:, p, k], k, KT)
                last.then_inc(wo_done, 1)

        def transposes(t):
            pe.wait_ge(xn_ready, TT * (t + 1))
            for k in range(KT):
                for a in range(TT):
                    last = nc.tensor.transpose(tr_ps[:, k, P * a:P * (a + 1)], xn[:, a, P * k:P * (k + 1)], ident[:])
                last.then_inc(xt_ps_ready, 1)

        def ffn_up(t, ms):
            pe.wait_ge(xt_lo, KT * (t + 1))
            for m in ms:
                wait(pe, gelu_done, MT * t + m - 1)
                for k in range(KT):
                    last = mm3(nc, hid_ps[:, m % 2], lambda p: w1[:, p, k, P * m:P * (m + 1)],
                               lambda p: xt[:, p, k], k, KT)
                last.then_inc(hid_done, 1)

        def ffn_down(t):
            wait(pe, y_ready, TT * t)
            for a in range(TT):
                for k in range(MT):
                    if a == 0:
                        pe.wait_ge(h_lo, MT * t + k + 1)
                    last = mm3(nc, y_ps[:, a // 2, (a % 2) * D:(a % 2 + 1) * D],
                               lambda p: h[:, p, k, P * a:P * (a + 1)], lambda p: w2[:, p, k], k, MT)
                last.then_inc(y_done, 1)

        def body(t, nxt=True, projected=False):
            ffn_up(t, range(2))
            if nxt and not projected:
                project(t + 1)
            ffn_up(t, range(2, MT))
            if nxt:
                transposes(t + 1)
            ffn_down(t)

        def main():
            pe.wait_ge(b.signals["o_ready"], 2 * NG)
            transposes(0)
            project(1)
            body(0, projected=True)
            with pe.Fori(1, NCH - 1) as t:
                body(t)
            body(NCH - 1, nxt=False)

        return {5 + a: lambda a=a: project(0, [a]) for a in range(TT)}, main

    return Programs(sync, gpsimd, scalar, vector, tensor)



def rope_tables():
    inv_freq = (np.float32(1.0) / np.float32(10000.0) ** (np.arange(0, 8, 2, dtype=np.float32) / np.float32(8)))
    ang = np.arange(S, dtype=np.float32)[None, :] * inv_freq.astype(np.float32)[:, None]
    rows = np.arange(P) % 4
    sign = np.where(np.arange(P) < P // 2, 1.0, -1.0).astype(np.float32)
    return np.cos(ang)[rows], np.sin(ang)[rows] * sign[:, None]


def kernel(**inputs):
    import concourse.bacc as bacc
    from concourse.bass_utils import run_bass_kernel_spmd

    a = {k[3:]: np.asarray(v) for k, v in inputs.items()}

    def rows(w):
        return w.reshape(H, 2, 4, D).transpose(1, 0, 2, 3).reshape(P, D)

    wqk = np.concatenate([rows(a[n]) for n in ("attn_Wq_sem", "attn_Wq_geo", "attn_Wk_sem", "attn_Wk_geo")])
    cos, sin = rope_tables()
    arrays = {
        "x": a["attn_x"].reshape(B * S, D),
        "w1t": a["ffn_proj1"].T, "w2t": a["ffn_proj2"].T, "wqkt": wqk.T, "wvt": a["attn_Wv"].T,
        "wot": a["attn_Wo"].T, "b1": a["ffn_proj1_bias"].reshape(MT, P).T, "b2": a["ffn_proj2_bias"],
        "cos": cos, "sin": sin,
    }
    arrays = {f"in_{k}": np.ascontiguousarray(v) for k, v in arrays.items()}
    nc = bacc.Bacc("TRN2", target_bir_lowering=False, num_devices=1)
    args = [nc.dram_tensor(k, v.shape, mybir.dt.from_np(v.dtype), kind="ExternalInput").ap() for k, v in arrays.items()]
    args.append(nc.dram_tensor("out_0", (B * S, D), F32, kind="ExternalOutput").ap())
    macaron(nc, *args)
    r = run_bass_kernel_spmd(nc, [arrays], core_ids=[0])
    return r.results[0]["out_0"].reshape(B, S, D)
```
